# Optimizing a Trainium2 kernel written in Bass

```python
import numpy as np
import jax
import jax.numpy as jnp

def _softmax(x, axis=-1):
    return jax.nn.softmax(x, axis=axis)

def _gelu(x):
    return jax.nn.gelu(x, approximate=True)

def _silu(x):
    return jax.nn.silu(x)

def _sigmoid(x):
    return jax.nn.sigmoid(x)

def _layernorm(x, axis=-1, eps=1e-05):
    m = jnp.mean(x, axis=axis, keepdims=True)
    v = jnp.var(x, axis=axis, keepdims=True)
    return (x - m) / jnp.sqrt(v + eps)

def _scatter_add(tgt, idx, src, axis=0):
    return tgt.at[idx].add(src)

def _segment_sum(src, seg, n):
    return jax.ops.segment_sum(src, seg, n)
kernel_name = 'mk_decoder_preln_d1_seqx_r8_bde9ad'

def setup_inputs(seed: int=0):
    np.random.seed(seed)
    _w = jnp.asarray

    def _rec_inputs():
        import jax
        import jax.numpy as jnp
        _rk = jax.random.key(seed)
        x = -0.0002928 + 1 * jax.random.normal(jax.random.fold_in(_rk, 1), (32, 128, 128), jnp.float32)
        _lenS = 128 - jax.random.randint(jax.random.fold_in(_rk, 7), (32,), 0, max(1, 128 // 4) + 1, jnp.int32)
        _lenS2 = 128 - jax.random.randint(jax.random.fold_in(_rk, 8), (32,), 0, max(1, 128 // 4) + 1, jnp.int32)
        _ctx_1024P = jax.random.normal(jax.random.fold_in(_rk, 11), (32, 16, 128), jnp.float32)
        _ctx_1024c = jax.random.dirichlet(jax.random.fold_in(_rk, 511), 0.3 * jnp.ones((16,), jnp.float32), (32, 128))
        _ctx_1024t = jnp.einsum('bsk,bkd->bsd', _ctx_1024c, _ctx_1024P)
        _ctx_1024t = _ctx_1024t * jax.lax.rsqrt(jnp.mean(jnp.square(_ctx_1024t)) + 1e-12) * 0.953939
        ctx_1024 = -1.39393e-06 + 0.999914 * (_ctx_1024t + 0.3 * jax.random.normal(jax.random.fold_in(_rk, 611), (32, 128, 128), jnp.float32))
        return (x, ctx_1024)
    x, ctx_1024 = _rec_inputs()

    def _L0_attn_setup():
        import jax, jax.numpy as jnp
        import numpy as np
        B, S, D_IN, D_OUT, H = (2, 256, 128, 128, 16)
        HD = D_OUT // H
        key = jax.random.key(seed)
        ks = jax.random.split(key, 6)
        x = jax.random.normal(ks[0], (B, S, D_IN), jnp.float32)
        Wq = jax.random.normal(ks[1], (D_IN, D_OUT), jnp.float32) * 0.02
        Wk = jax.random.normal(ks[2], (D_IN, D_OUT), jnp.float32) * 0.02
        Wv = jax.random.normal(ks[3], (D_IN, D_OUT), jnp.float32) * 0.02
        Wo = jax.random.normal(ks[4], (D_OUT, D_OUT), jnp.float32) * 0.02
        bo = jax.random.normal(ks[5], (D_OUT,), jnp.float32) * 0.02
        return {'x': x, 'Wq': Wq, 'Wk': Wk, 'Wv': Wv, 'Wo': Wo, 'bo': bo}
    _L0_attn_all = _L0_attn_setup()
    _L0_attn_in = {k: v for k, v in _L0_attn_all.items() if k in ('Wq', 'Wk', 'Wv', 'Wo', 'bo')}
    del _L0_attn_all

    def _L0_xattn_setup():
        import jax, jax.numpy as jnp
        import numpy as np
        HEADS = 16

        def _attn(q, k, v, Wq, Wk, Wv, Wo):
            b, n, dim = q.shape
            h = HEADS
            qp = q @ Wq
            kp = k @ Wk
            vp = v @ Wv

            def split_heads(t):
                return t.reshape(b, n, h, -1).transpose(0, 2, 1, 3)
            qh, kh, vh = map(split_heads, (qp, kp, vp))
            scale = qh.shape[-1] ** (-0.5)
            qh = qh * scale
            sim = jnp.einsum('bhid,bhjd->bhij', qh, kh)
            attn = jax.nn.softmax(sim, axis=-1)
            out = jnp.einsum('bhij,bhjd->bhid', attn, vh)
            out = out.transpose(0, 2, 1, 3).reshape(b, n, -1)
            return out @ Wo
        key = jax.random.key(seed)
        ks = jax.random.split(key, 7)
        b, n, dim = (2, 256, 128)
        inner = HEADS * 64
        s = dim ** (-0.5)
        return {'q': jax.random.normal(ks[0], (b, n, dim), jnp.float32), 'k': jax.random.normal(ks[1], (b, n, dim), jnp.float32), 'v': jax.random.normal(ks[2], (b, n, dim), jnp.float32), 'Wq': jax.random.normal(ks[3], (dim, inner), jnp.float32) * s, 'Wk': jax.random.normal(ks[4], (dim, inner), jnp.float32) * s, 'Wv': jax.random.normal(ks[5], (dim, inner), jnp.float32) * s, 'Wo': jax.random.normal(ks[6], (inner, dim), jnp.float32) * s}
    _L0_xattn_all = _L0_xattn_setup()
    _L0_xattn_in = {k: v for k, v in _L0_xattn_all.items() if k in ('Wq', 'Wk', 'Wv', 'Wo')}
    del _L0_xattn_all

    def _L0_ffn_setup():
        import jax, jax.numpy as jnp
        import numpy as np
        DIM = 128
        DEPTH = 6
        HEADS = 16
        DIM_HEAD = 64
        WINDOW = 32
        INNER = HEADS * DIM_HEAD
        DIM_INNER = int(DIM * 4 * 2 / 3)
        QK_SCALE = 8.0

        def shift_tokens(t):
            a, s = jnp.split(t, 2, -1)
            s = jnp.pad(s, ((0, 0), (1, 0), (0, 0)))[:, :-1]
            return jnp.concatenate([a, s], -1)

        def l2norm(t):
            return t / jnp.maximum(jnp.linalg.norm(t, axis=-1, keepdims=True), 1e-12)

        def rotate_half(x):
            x1, x2 = jnp.split(x, 2, -1)
            return jnp.concatenate([-x2, x1], -1)

        def rotary_tables(n):
            half = jnp.arange(0, DIM_HEAD, 2, dtype=jnp.float32)
            inv_freq = 1.0 / 10000.0 ** (half / DIM_HEAD)
            t = jnp.arange(n, dtype=jnp.float32)
            freqs = t[:, None] * inv_freq[None, :]
            freqs = jnp.concatenate([freqs, freqs], -1)
            base_scale = (half + 0.4 * DIM_HEAD) / (1.4 * DIM_HEAD)
            power = (t - n // 2) / (WINDOW // 2)
            scale = base_scale[None, :] ** power[:, None]
            scale = jnp.concatenate([scale, scale], -1)
            return (freqs, scale)

        def local_attention(q, k, v):
            b, h, n, d = q.shape
            w = WINDOW
            nw = n // w
            bq = q.reshape(b, h, nw, w, d)
            bk = k.reshape(b, h, nw, w, d)
            bv = v.reshape(b, h, nw, w, d)

            def look(t):
                p = jnp.pad(t, ((0, 0), (0, 0), (1, 0), (0, 0), (0, 0)))
                return jnp.concatenate([p[:, :, :nw], p[:, :, 1:]], axis=3)
            bk2, bv2 = (look(bk), look(bv))
            seq = jnp.arange(n).reshape(nw, w)
            seq_p = jnp.pad(seq, ((1, 0), (0, 0)), constant_values=-1)
            jt = jnp.concatenate([seq_p[:nw], seq_p[1:]], axis=1)
            it = seq[:, :, None]
            jb = jt[:, None, :]
            mask = (it < jb) | (it > jb + w) | (jb == -1)
            sim = jnp.einsum('bhwie,bhwje->bhwij', bq, bk2) * QK_SCALE
            sim = jnp.where(mask, -jnp.finfo(sim.dtype).max, sim)
            attn = jax.nn.softmax(sim, -1)
            out = jnp.einsum('bhwij,bhwje->bhwie', attn, bv2)
            return out.reshape(b, h, n, d)

        def attn_layer(x, Wqkv, qs, ksc, Wo):
            b, n, _ = x.shape
            qkv = x @ Wqkv
            q, k, v = jnp.split(qkv, 3, -1)
            sh = lambda t: t.reshape(b, n, HEADS, DIM_HEAD).transpose(0, 2, 1, 3)
            q, k, v = (sh(q), sh(k), sh(v))
            q = l2norm(q) * qs
            k = l2norm(k) * ksc
            freqs, scale = rotary_tables(n)
            cos, sin = (jnp.cos(freqs), jnp.sin(freqs))
            q = q * cos * scale + rotate_half(q) * sin * scale
            inv = 1.0 / scale
            k = k * cos * inv + rotate_half(k) * sin * inv
            out = local_attention(q, k, v)
            out = out.transpose(0, 2, 1, 3).reshape(b, n, INNER)
            return out @ Wo

        def ffn_layer(x, g, bln, W1, b1, W2, b2):
            mu = x.mean(-1, keepdims=True)
            var = ((x - mu) ** 2).mean(-1, keepdims=True)
            xn = (x - mu) / jnp.sqrt(var + 1e-05) * g + bln
            hg = xn @ W1 + b1
            a, gate = jnp.split(hg, 2, -1)
            return a * jax.nn.gelu(gate, approximate=False) @ W2 + b2
        key = jax.random.key(seed)
        ks = jax.random.split(key, 8)
        B, N = (2, 256)
        init = lambda k, shape: jax.random.normal(k, shape, jnp.float32) * 0.02
        return {'x': jax.random.normal(ks[0], (B, N, DIM), jnp.float32), 'Wqkv': init(ks[1], (DEPTH, DIM, 3 * INNER)), 'q_scale': jnp.ones((DEPTH, DIM_HEAD), jnp.float32), 'k_scale': jnp.ones((DEPTH, DIM_HEAD), jnp.float32), 'Wo': init(ks[2], (DEPTH, INNER, DIM)), 'ln_g': jnp.ones((DEPTH, DIM), jnp.float32), 'ln_b': jnp.zeros((DEPTH, DIM), jnp.float32), 'W1': init(ks[3], (DEPTH, DIM, 2 * DIM_INNER)), 'b1': jnp.zeros((DEPTH, 2 * DIM_INNER), jnp.float32), 'W2': init(ks[4], (DEPTH, DIM_INNER, DIM)), 'b2': jnp.zeros((DEPTH, DIM), jnp.float32)}
    _L0_ffn_all = _L0_ffn_setup()
    _L0_ffn_in = {k: v for k, v in _L0_ffn_all.items() if k in ('Wqkv', 'q_scale', 'k_scale', 'Wo', 'ln_g', 'ln_b', 'W1', 'b1', 'W2', 'b2')}
    del _L0_ffn_all
    return {'x': x, 'ctx_1024': ctx_1024, 'L0_attn_Wq': _L0_attn_in['Wq'], 'L0_attn_Wk': _L0_attn_in['Wk'], 'L0_attn_Wv': _L0_attn_in['Wv'], 'L0_attn_Wo': _L0_attn_in['Wo'], 'L0_attn_bo': _L0_attn_in['bo'], 'L0_xattn_Wq': _L0_xattn_in['Wq'], 'L0_xattn_Wk': _L0_xattn_in['Wk'], 'L0_xattn_Wv': _L0_xattn_in['Wv'], 'L0_xattn_Wo': _L0_xattn_in['Wo'], 'L0_ffn_Wqkv': _L0_ffn_in['Wqkv'], 'L0_ffn_q_scale': _L0_ffn_in['q_scale'], 'L0_ffn_k_scale': _L0_ffn_in['k_scale'], 'L0_ffn_Wo': _L0_ffn_in['Wo'], 'L0_ffn_ln_g': _L0_ffn_in['ln_g'], 'L0_ffn_ln_b': _L0_ffn_in['ln_b'], 'L0_ffn_W1': _L0_ffn_in['W1'], 'L0_ffn_b1': _L0_ffn_in['b1'], 'L0_ffn_W2': _L0_ffn_in['W2'], 'L0_ffn_b2': _L0_ffn_in['b2']}

def reference(x, ctx_1024, L0_attn_Wq, L0_attn_Wk, L0_attn_Wv, L0_attn_Wo, L0_attn_bo, L0_xattn_Wq, L0_xattn_Wk, L0_xattn_Wv, L0_xattn_Wo, L0_ffn_Wqkv, L0_ffn_q_scale, L0_ffn_k_scale, L0_ffn_Wo, L0_ffn_ln_g, L0_ffn_ln_b, L0_ffn_W1, L0_ffn_b1, L0_ffn_W2, L0_ffn_b2):
    import jax
    import jax.numpy as jnp

    def _L0_attn_ref(x, Wq, Wk, Wv, Wo, bo):
        import jax, jax.numpy as jnp
        import numpy as np
        B, S, D_IN, D_OUT, H = (2, 256, 128, 128, 16)
        HD = D_OUT // H
        b, s, _ = x.shape

        def to_heads(t):
            return t.reshape(b, s, H, HD).transpose(0, 2, 1, 3)
        Q = to_heads(x @ Wq)
        K = to_heads(x @ Wk)
        V = to_heads(x @ Wv)
        scale = 1.0 / jnp.sqrt(jnp.asarray(HD, x.dtype))
        scores = jnp.einsum('bhqd,bhkd->bhqk', Q, K) * scale
        causal_mask = jnp.triu(jnp.ones((s, s), dtype=bool), k=1)
        scores = jnp.where(causal_mask, jnp.asarray(-1000000.0, scores.dtype), scores)
        weights = jax.nn.softmax(scores, axis=-1)
        attn = jnp.einsum('bhqk,bhkd->bhqd', weights, V)
        attn = attn.reshape(b, s, D_OUT)
        return attn @ Wo + bo

    def _L0_xattn_ref(q, k, v, Wq, Wk, Wv, Wo):
        import jax, jax.numpy as jnp
        import numpy as np
        HEADS = 16

        def _attn(q, k, v, Wq, Wk, Wv, Wo):
            b, n, dim = q.shape
            h = HEADS
            qp = q @ Wq
            kp = k @ Wk
            vp = v @ Wv

            def split_heads(t):
                return t.reshape(b, n, h, -1).transpose(0, 2, 1, 3)
            qh, kh, vh = map(split_heads, (qp, kp, vp))
            scale = qh.shape[-1] ** (-0.5)
            qh = qh * scale
            sim = jnp.einsum('bhid,bhjd->bhij', qh, kh)
            attn = jax.nn.softmax(sim, axis=-1)
            out = jnp.einsum('bhij,bhjd->bhid', attn, vh)
            out = out.transpose(0, 2, 1, 3).reshape(b, n, -1)
            return out @ Wo
        return _attn(q, k, v, Wq, Wk, Wv, Wo)

    def _L0_ffn_ref(x, Wqkv, q_scale, k_scale, Wo, ln_g, ln_b, W1, b1, W2, b2):
        import jax, jax.numpy as jnp
        import numpy as np
        DIM = 128
        DEPTH = 6
        HEADS = 16
        DIM_HEAD = 64
        WINDOW = 32
        INNER = HEADS * DIM_HEAD
        DIM_INNER = int(DIM * 4 * 2 / 3)
        QK_SCALE = 8.0

        def shift_tokens(t):
            a, s = jnp.split(t, 2, -1)
            s = jnp.pad(s, ((0, 0), (1, 0), (0, 0)))[:, :-1]
            return jnp.concatenate([a, s], -1)

        def l2norm(t):
            return t / jnp.maximum(jnp.linalg.norm(t, axis=-1, keepdims=True), 1e-12)

        def rotate_half(x):
            x1, x2 = jnp.split(x, 2, -1)
            return jnp.concatenate([-x2, x1], -1)

        def rotary_tables(n):
            half = jnp.arange(0, DIM_HEAD, 2, dtype=jnp.float32)
            inv_freq = 1.0 / 10000.0 ** (half / DIM_HEAD)
            t = jnp.arange(n, dtype=jnp.float32)
            freqs = t[:, None] * inv_freq[None, :]
            freqs = jnp.concatenate([freqs, freqs], -1)
            base_scale = (half + 0.4 * DIM_HEAD) / (1.4 * DIM_HEAD)
            power = (t - n // 2) / (WINDOW // 2)
            scale = base_scale[None, :] ** power[:, None]
            scale = jnp.concatenate([scale, scale], -1)
            return (freqs, scale)

        def local_attention(q, k, v):
            b, h, n, d = q.shape
            w = WINDOW
            nw = n // w
            bq = q.reshape(b, h, nw, w, d)
            bk = k.reshape(b, h, nw, w, d)
            bv = v.reshape(b, h, nw, w, d)

            def look(t):
                p = jnp.pad(t, ((0, 0), (0, 0), (1, 0), (0, 0), (0, 0)))
                return jnp.concatenate([p[:, :, :nw], p[:, :, 1:]], axis=3)
            bk2, bv2 = (look(bk), look(bv))
            seq = jnp.arange(n).reshape(nw, w)
            seq_p = jnp.pad(seq, ((1, 0), (0, 0)), constant_values=-1)
            jt = jnp.concatenate([seq_p[:nw], seq_p[1:]], axis=1)
            it = seq[:, :, None]
            jb = jt[:, None, :]
            mask = (it < jb) | (it > jb + w) | (jb == -1)
            sim = jnp.einsum('bhwie,bhwje->bhwij', bq, bk2) * QK_SCALE
            sim = jnp.where(mask, -jnp.finfo(sim.dtype).max, sim)
            attn = jax.nn.softmax(sim, -1)
            out = jnp.einsum('bhwij,bhwje->bhwie', attn, bv2)
            return out.reshape(b, h, n, d)

        def attn_layer(x, Wqkv, qs, ksc, Wo):
            b, n, _ = x.shape
            qkv = x @ Wqkv
            q, k, v = jnp.split(qkv, 3, -1)
            sh = lambda t: t.reshape(b, n, HEADS, DIM_HEAD).transpose(0, 2, 1, 3)
            q, k, v = (sh(q), sh(k), sh(v))
            q = l2norm(q) * qs
            k = l2norm(k) * ksc
            freqs, scale = rotary_tables(n)
            cos, sin = (jnp.cos(freqs), jnp.sin(freqs))
            q = q * cos * scale + rotate_half(q) * sin * scale
            inv = 1.0 / scale
            k = k * cos * inv + rotate_half(k) * sin * inv
            out = local_attention(q, k, v)
            out = out.transpose(0, 2, 1, 3).reshape(b, n, INNER)
            return out @ Wo

        def ffn_layer(x, g, bln, W1, b1, W2, b2):
            mu = x.mean(-1, keepdims=True)
            var = ((x - mu) ** 2).mean(-1, keepdims=True)
            xn = (x - mu) / jnp.sqrt(var + 1e-05) * g + bln
            hg = xn @ W1 + b1
            a, gate = jnp.split(hg, 2, -1)
            return a * jax.nn.gelu(gate, approximate=False) @ W2 + b2
        for i in range(DEPTH):
            x = attn_layer(shift_tokens(x), Wqkv[i], q_scale[i], k_scale[i], Wo[i]) + x
            x = ffn_layer(shift_tokens(x), ln_g[i], ln_b[i], W1[i], b1[i], W2[i], b2[i]) + x
        return x
    x = x + _L0_attn_ref(_layernorm(x, axis=-1), L0_attn_Wq, L0_attn_Wk, L0_attn_Wv, L0_attn_Wo, L0_attn_bo)
    x = x + _L0_xattn_ref(_layernorm(x, axis=-1), ctx_1024, ctx_1024, L0_xattn_Wq, L0_xattn_Wk, L0_xattn_Wv, L0_xattn_Wo)
    x = x + _L0_ffn_ref(_layernorm(x, axis=-1), L0_ffn_Wqkv, L0_ffn_q_scale, L0_ffn_k_scale, L0_ffn_Wo, L0_ffn_ln_g, L0_ffn_ln_b, L0_ffn_W1, L0_ffn_b1, L0_ffn_W2, L0_ffn_b2)
    return x

_drawn_inputs = setup_inputs


def setup_inputs(seed=0):
    import zlib

    import numpy as np

    out = dict(_drawn_inputs(seed))
    spreads = {'L0_ffn_q_scale': (1.0, 0.6),
     'L0_ffn_k_scale': (1.0, 0.6),
     'L0_ffn_ln_g': (1.0, 0.6),
     'L0_ffn_ln_b': (0.0, 0.8),
     'L0_ffn_b1': (0.0, 0.8),
     'L0_ffn_b2': (0.0, 0.1)}
    factors = {'L0_attn_Wq': 8.0,
     'L0_attn_Wk': 8.0,
     'L0_attn_Wv': 8.0,
     'L0_attn_Wo': 8.0,
     'L0_attn_bo': 3.718,
     'L0_ffn_W1': 5.158,
     'L0_ffn_W2': 5.097}
    for name, (base, spread) in spreads.items():
        noise = np.random.default_rng([zlib.crc32(name.encode()), seed]).standard_normal(out[name].shape)
        drawn = base * np.exp(spread * noise) if base else spread * noise
        out[name] = jnp.asarray(drawn.astype(out[name].dtype))
    for name, factor in factors.items():
        out[name] = (out[name] * factor).astype(out[name].dtype)
    return out
```

```python
import concourse.bass as bass
from concourse import mybir
from contextlib import ExitStack

FP32 = mybir.dt.float32
BF16 = mybir.dt.bfloat16
I32 = mybir.dt.int32
ALU = mybir.AluOpType
ACT = mybir.ActivationFunctionType
AX = mybir.AxisListType

UNITS = 32
T = 128
D = 128
H = 16
GH = 4
NG = H // GH
DH = 64
INNER = H * DH
DH_SELF = D // H
QK_SCALE = 8
LAYERS = 6
FF = 341
FC = [128, 128, FF - 256]
BANK = 512
QKV_CHUNKS = 3 * INNER // BANK
FB = 4
NFB = UNITS // FB
EPS = 1e-5
CREDIT = 2
MAX_LAG = {"self": 4, "cross": 4, "local": 2, "ff": 2}
NEWTON = 3
MAGIC = 0x5F3759DF

WO_AT = 3 * INNER
ATTN_COLS = WO_AT + (INNER // 128) * D
W2_AT = 2 * FF
B1_AT = W2_AT + 3 * D
G_AT = B1_AT + 6
B2_AT = G_AT + 2
FFN_COLS = B2_AT + D


class Counter:

    def __init__(self, sem, per_unit):
        self.sem, self.k = sem, per_unit

    def of(self, n, step):
        return (n + CREDIT) * self.k + step

    def before(self, n, step, back=1):
        return (n + (CREDIT - back)) * self.k + step


def build(nc, x, ctx_in, self_w, self_bo, cross_w, attn_w, qk_scale, ffn_w, ident_in, shift_in,
          rot_in, headmask_in, masks_in, out):
    stack = ExitStack()
    with stack:
        def sb(name, shape, dt=FP32):
            return stack.enter_context(nc.sbuf_tensor(name, shape, dt))

        def sem(name):
            return stack.enter_context(nc.semaphore(name))

        XA = sb("XA", [T, UNITS * D])
        XB = sb("XB", [T, UNITS * D])
        CTX = sb("CTX", [T, UNITS * D])
        W = sb("W", [128, ATTN_COLS])
        WF = sb("WF", [128, FFN_COLS])
        BO = sb("BO", [1, D])
        ident = sb("ident", [128, 128])
        shift = sb("shift", [128, 128])
        identb = sb("identb", [128, 128], BF16)
        masks = sb("masks", [128, 2 * T], BF16)
        masks_f = sb("masks_f", [128, 2 * T])
        headmask = sb("headmask", [128, H])
        rot = sb("rot", [T, 4 * DH])
        scl = sb("scl", [T, LAYERS * 2 * DH])
        tab = sb("tab", [T, 4 * DH])
        ones = sb("ones", [1, 128])
        powc = sb("powc", [T, 32])
        three_halves = sb("three_halves", [T, 2 * H])
        xa = sb("xa", [T, 2 * D])
        yT = sb("yT", [D, 2 * T])
        sq = sb("sq", [T, 2 * BANK])
        tu = sb("tu", [T, 2 * 2 * BANK])
        n2 = sb("n2", [T, 2 * H])
        n2c = sb("n2c", [T, 2 * H])
        n2h = sb("n2h", [T, 2 * H])
        half_bits = sb("half_bits", [T, 2 * H], I32)
        guess = sb("guess", [T, 2 * H])
        newt = sb("newt", [T, 2 * H])
        rn = sb("rn", [T, 2 * 2 * H])
        rsb = sb("rsb", [T, 2 * INNER])
        knb = sb("knb", [T, INNER])
        QP = sb("QP", [128, 2 * H * T])
        KT = sb("KT", [128, 2 * 8 * T])
        V = sb("V", [T, 2 * H * D])
        P = sb("P", [T, H * T])
        mx = sb("mx", [T, H])
        nb = sb("nb", [T, H])
        rs = sb("rs", [T, H])
        ri = sb("ri", [T, H])
        PTs = sb("PTs", [T, 2 * BANK])
        OT = sb("OT", [128, 8 * T])
        stats = sb("stats", [T, UNITS * 6])
        mv = sb("mv", [T, UNITS * 2])
        rstd = sb("rstd", [T, UNITS])
        xc = sb("xc", [T, FB * D])
        xn = sb("xn", [T, FB * D])
        xnT = sb("xnT", [D, 2 * FB * T])
        gel = sb("gel", [128, 3 * BANK])
        gT = sb("gT", [128, 3 * BANK])

        banks = [stack.enter_context(nc.psum_tensor(f"bank{i}", [128, BANK], FP32)) for i in range(8)]
        PROJ = banks[0:2]
        TRP, YPS = banks[2], banks[3]
        SPS = banks[4:6]
        PTP, OTP = banks[6], banks[7]

        consts_in = sem("consts_in")
        x_in = sem("x_in")
        ctx_sem = sem("ctx_in")
        selfw_in = sem("selfw_in")
        attnw_in = sem("attnw_in")
        ffnw_in = sem("ffnw_in")
        out_sem = sem("out_sem")
        const_made = sem("const_made")
        bf_made = sem("bf_made")
        held = sem("held")
        pass_done = sem("pass_done")
        ln_step = sem("ln_step")
        ln_stats = sem("ln_stats")
        ln_eps = sem("ln_eps")
        ln_rstd = sem("ln_rstd")
        tab_made = sem("tab_made")
        qp_zero = sem("qp_zero")

        class Counters:

            def __init__(self, kind):
                def c(what, per_unit=1):
                    return Counter(sem(f"{kind}_{what}"), per_unit)

                local, alone = kind == "local", kind == "self"
                self.xT_ps, self.proj_ps = c("xT_ps"), c("proj_ps", QKV_CHUNKS)
                self.scores, self.probT_ps = c("scores", NG), c("probT_ps", NG)
                self.av_ps, self.y_ps = c("av_ps", NG), c("y_ps")
                self.tensor = [self.xT_ps, self.proj_ps, self.scores, self.probT_ps, self.av_ps, self.y_ps]
                self.yT_sb, self.prob = c("yT_sb"), c("prob", NG)
                self.scalar = [self.yT_sb, self.prob]
                self.rowmax, self.negmax = c("rowmax", NG), c("negmax", NG)
                self.recip, self.updated = c("recip", NG), c("updated")
                self.vector = [self.rowmax, self.negmax, self.recip, self.updated]
                self.staged, self.probn = c("staged"), c("probn", NG)
                self.pool = [self.staged, self.probn]
                self.probT = c("probT", NG)
                (self.scalar if alone else self.vector).append(self.probT)
                if alone:
                    self.selfk, self.selfv = c("selfk"), c("selfv")
                    self.scalar += [self.selfk, self.selfv]
                    self.selfq, self.picked, self.selfo = c("selfq"), c("picked", NG), c("selfo", NG)
                    self.vector += [self.selfq, self.picked, self.selfo]
                else:
                    self.qk_sb, self.v_sb, self.oT_sb = c("qk_sb", 4), c("v_sb", 2), c("oT_sb", 2)
                    self.scalar += [self.qk_sb, self.v_sb, self.oT_sb]
                if local:
                    self.trans_ps = c("trans_ps", 4)
                    self.tensor.append(self.trans_ps)
                    self.squared = c("squared", 4)
                    self.scalar.append(self.squared)
                    self.rotated, self.norm2 = c("rotated", 4), c("norm2", 4)
                    self.seeded, self.knorm = c("seeded", 3), c("knorm", 2)
                    self.vector += [self.rotated, self.norm2, self.seeded, self.knorm]
                    self.rsum, self.newton = c("rsum", 4), c("newton", 4 * NEWTON)
                    self.pool += [self.rsum, self.newton]

        CS, CC, CL = Counters("self"), Counters("cross"), Counters("local")

        def give_credit(eng, counted):
            for c in counted:
                eng.sem_inc(c.sem, CREDIT * c.k)

        class FeedForwardCounters:
            def __init__(self):
                def c(what, per_block=1):
                    return Counter(sem(f"ff_{what}"), per_block)

                self.shift_ps, self.xnT_ps, self.up_ps, self.down_ps = c("shift_ps"), c("xnT_ps"), c("up_ps", 3), c("down_ps")
                self.tensor = [self.shift_ps, self.xnT_ps, self.up_ps, self.down_ps]
                self.xnT, self.gelu = c("xnT"), c("gelu", 3)
                self.scalar = [self.xnT, self.gelu]
                self.bn1, self.bn2, self.cent, self.xn = c("bn1"), c("bn2"), c("cent"), c("xn")
                self.gate, self.upd = c("gate", 3), c("upd")
                self.vector = [self.bn1, self.bn2, self.cent, self.xn, self.gate, self.upd]
                self.eps, self.rstd = c("eps"), c("rstd")
                self.pool = [self.eps, self.rstd]

        CF = FeedForwardCounters()

        class Unit:
            def __init__(self, n, u, p):
                self.n, self.u, self.p = n, u, p

        class Turn:

            def __init__(self, base, v, parity, first=0, last=0):
                self.base, self.v, self.parity, self.first, self.last = base, v, parity, first, last

            def run(self, operation, lag, *part):
                if lag < self.first or lag > self.last:
                    return
                u = self.v - lag
                operation(Unit(self.base + u, u, (self.parity + lag) % 2), *part)

        def pipeline(eng, base, turn, lags, units=UNITS):
            for v in range(lags):
                turn(Turn(base, v, v % 2, last=v))
            hold(eng)
            with eng.Fori(0, (units - lags) // 2) as j:
                for p in range(2):
                    turn(Turn(base, j * 2 + (lags + p), p, last=lags))
            for v in range(units, units + lags):
                turn(Turn(base, v, v % 2, first=v - units + 1, last=lags))

        def cols(t, at, n):
            return t[:, bass.ds(at, n)]

        def hold(eng):
            eng.sem_inc(held, 1)

        PASSES_BEFORE_LAYERS = 5

        block = stack.enter_context(nc.Block())

        @block.sync
        def _(sp):
            sp.dma_start(XA[:, :].rearrange("t (b d) -> t b d", d=D), x.rearrange("b t d -> t b d")).then_inc(x_in, 16)
            for dst, src in ((ident, ident_in), (shift, shift_in), (rot, rot_in), (headmask, headmask_in),
                             (masks_f, masks_in)):
                sp.dma_start(dst[:, :], src).then_inc(consts_in, 16)
            sp.dma_start(WF[:, 0:4 * D], self_w).then_inc(selfw_in, 16)
            sp.dma_start(BO[:, :], self_bo).then_inc(selfw_in, 16)
            sp.dma_start(scl[:, :], qk_scale.to_broadcast([T, LAYERS * 2 * DH])).then_inc(consts_in, 16)
            sp.dma_start(W[:, :], cross_w).then_inc(attnw_in, 16)
            sp.dma_start(CTX[:, :].rearrange("t (b d) -> t b d", d=D), ctx_in.rearrange("b t d -> t b d")).then_inc(ctx_sem, 16)
            sp.wait_ge(pass_done, 2)
            sp.dma_start(WF[:, :], ffn_w[0]).then_inc(ffnw_in, 16)
            sp.wait_ge(pass_done, 4)
            sp.dma_start(W[:, :], attn_w[0]).then_inc(attnw_in, 16)
            with sp.Fori(1, LAYERS) as l:
                sp.wait_ge(pass_done, l * 2 + (PASSES_BEFORE_LAYERS - 1))
                sp.dma_start(W[:, :], attn_w[bass.ds(l, 1)].rearrange("o p n -> p (o n)")).then_inc(attnw_in, 16)
                sp.wait_ge(pass_done, l * 2 + PASSES_BEFORE_LAYERS)
                sp.dma_start(WF[:, :], ffn_w[bass.ds(l, 1)].rearrange("o p n -> p (o n)")).then_inc(ffnw_in, 16)
            sp.wait_ge(pass_done, PASSES_BEFORE_LAYERS + 2 * LAYERS + 1)
            sp.dma_start(out.rearrange("b t d -> t b d"), XA[:, :].rearrange("t (b d) -> t b d", d=D)).then_inc(out_sem, 16)
            sp.wait_ge(out_sem, 16)

        @block.gpsimd
        def _(pool):
            give_credit(pool, CS.pool + CC.pool + CL.pool)
            give_credit(pool, CF.pool)
            pool.memset(powc[:, :], -0.5).then_inc(const_made, 1)
            pool.memset(ones[:, :], 1.0).then_inc(const_made, 1)
            pool.memset(yT[:, :], 0.0).then_inc(const_made, 1)
            pool.memset(three_halves[:, :], 1.5).then_inc(const_made, 1)
            pool.wait_ge(const_made, 4)

            def norm_pass(k):
                pool.wait_ge(ln_stats, k)
                mvv = mv[:, :].rearrange("t (u two) -> t u two", two=2)
                pool.tensor_scalar(rstd[:, :], mvv[:, :, 1], EPS, None, ALU.add).then_inc(ln_eps, 1)
                pool.wait_ge(ln_eps, k)
                pool.tensor_tensor(rstd[:, :], rstd[:, :], powc[:, :], ALU.pow).then_inc(ln_rstd, 1)

            def attention(C, kind, base, src, after):
                pool.wait_ge(pass_done, after)
                if kind == "cross":
                    pool.memset(QP[:, :], 0.0).then_inc(qp_zero, 1)
                    pool.wait_ge(ctx_sem, 16)

                def stage(w):
                    n, u = w.n, w.u
                    pool.wait_ge(C.xT_ps.sem, C.xT_ps.before(n, 1))
                    hold(pool)
                    i = pool.tensor_copy(xa[:, 0:D], cols(src, u * D, D))
                    if kind == "cross":
                        i = pool.tensor_copy(xa[:, D:2 * D], cols(CTX, u * D, D))
                    i.then_inc(C.staged.sem, 1)

                def rotate_sum(w, c):
                    n = w.n
                    pool.wait_ge(C.rotated.sem, C.rotated.of(n, c + 1))
                    if c < 2:
                        pool.wait_ge(C.trans_ps.sem, C.trans_ps.before(n, c + 1))
                    else:
                        pool.wait_ge(C.knorm.sem, C.knorm.before(n, c - 1))
                    t = tu[:, (c % 2) * 2 * BANK:(c % 2 + 1) * 2 * BANK].rearrange(
                        "t (w h s d) -> t w h s d", w=2, h=8, s=2)
                    r = rsb[:, c * BANK:(c + 1) * BANK].rearrange("t (h s d) -> t h s d", h=8, s=2)
                    pool.tensor_tensor(r[:, :, 0, :], t[:, 0, :, 0, :], t[:, 1, :, 1, :], ALU.add)
                    pool.tensor_tensor(r[:, :, 1, :], t[:, 0, :, 1, :], t[:, 1, :, 0, :], ALU.add)\
                        .then_inc(C.rsum.sem, 1)

                def rnorm(w):
                    n, p = w.n, w.p
                    pool.wait_ge(C.seeded.sem, C.seeded.of(n, 3))
                    y = guess[:, :]
                    for i in range(NEWTON):
                        if i:
                            pool.wait_ge(C.newton.sem, C.newton.of(n, 4 * i))
                        pool.tensor_tensor(newt[:, :], y, y, ALU.mult).then_inc(C.newton.sem, 1)
                        pool.wait_ge(C.newton.sem, C.newton.of(n, 4 * i + 1))
                        pool.tensor_tensor(newt[:, :], newt[:, :], n2h[:, :], ALU.mult).then_inc(C.newton.sem, 1)
                        pool.wait_ge(C.newton.sem, C.newton.of(n, 4 * i + 2))
                        pool.tensor_tensor(newt[:, :], newt[:, :], three_halves[:, :], ALU.add).then_inc(C.newton.sem, 1)
                        dst = y
                        if i == NEWTON - 1:
                            dst = rn[:, p * 2 * H:(p + 1) * 2 * H]
                            pool.wait_ge(C.prob.sem, C.prob.before(n, NG, 2))
                            pool.wait_ge(C.knorm.sem, C.knorm.before(n, 2, 2))
                        pool.wait_ge(C.newton.sem, C.newton.of(n, 4 * i + 3))
                        pool.tensor_tensor(dst, y, newt[:, :], ALU.mult).then_inc(C.newton.sem, 1)

                def normalise(w, g):
                    n = w.n
                    pool.wait_ge(C.recip.sem, C.recip.of(n, g + 1))
                    pv = P[:, g * BANK:(g + 1) * BANK].rearrange("t (h k) -> t h k", h=GH)
                    pool.tensor_tensor(pv, pv, ri[:, g * GH:(g + 1) * GH].unsqueeze(2).to_broadcast([T, GH, T]),
                                       ALU.mult).then_inc(C.probn.sem, 1)

                def turn_self(t):
                    t.run(stage, 0)
                    t.run(normalise, 3, 0)
                    t.run(normalise, 3, 1)
                    t.run(normalise, 3, 2)
                    t.run(normalise, 3, 3)

                def turn_cross(t):
                    t.run(normalise, 3, 1)
                    t.run(normalise, 3, 2)
                    t.run(stage, 0)
                    t.run(normalise, 3, 3)
                    t.run(normalise, 2, 0)

                def turn_local(t):
                    t.run(rotate_sum, 1, 0)
                    t.run(stage, 0)
                    t.run(rotate_sum, 1, 1)
                    t.run(normalise, 2, 0)
                    t.run(rotate_sum, 1, 2)
                    t.run(rnorm, 1)
                    t.run(rotate_sum, 1, 3)
                    t.run(normalise, 2, 1)
                    t.run(normalise, 2, 2)
                    t.run(normalise, 2, 3)

                turn_of_kind = {"self": turn_self, "cross": turn_cross, "local": turn_local}[kind]
                pipeline(pool, base, turn_of_kind, MAX_LAG[kind])

            norm_pass(1)
            attention(CS, "self", 0, XB, 1)
            norm_pass(2)
            attention(CC, "cross", 0, XB, 3)
            norm_pass(3)
            pool.wait_ge(pass_done, PASSES_BEFORE_LAYERS)
            pool.memset(yT[64:128, 0:1], 0.0).then_inc(const_made, 1)
            pool.wait_ge(const_made, 5)
            with pool.Fori(0, LAYERS) as l:
                attention(CL, "local", l * UNITS, XB, l * 2 + PASSES_BEFORE_LAYERS)
                pool.wait_ge(pass_done, l * 2 + (PASSES_BEFORE_LAYERS + 1))
                hold(pool)

                def make_rstd(w):
                    m = w.n
                    pool.wait_ge(CF.bn2.sem, CF.bn2.of(m, 1))
                    pool.wait_ge(CF.xn.sem, CF.xn.before(m, 1))
                    hold(pool)
                    mvv = mv[:, 0:2 * FB].rearrange("t (u two) -> t u two", two=2)
                    pool.tensor_scalar(rstd[:, 0:FB], mvv[:, :, 1], EPS, None, ALU.add).then_inc(CF.eps.sem, 1)
                    pool.wait_ge(CF.eps.sem, CF.eps.of(m, 1))
                    pool.tensor_tensor(rstd[:, 0:FB], rstd[:, 0:FB], powc[:, 0:FB], ALU.pow).then_inc(CF.rstd.sem, 1)

                def turn_ff(t):
                    t.run(make_rstd, 0)
                pipeline(pool, l * NFB, turn_ff, MAX_LAG["ff"], NFB)

        @block.scalar
        def _(act):
            give_credit(act, CS.scalar + CC.scalar + CL.scalar)
            give_credit(act, CF.scalar)
            act.wait_ge(const_made, 4)

            def attention(C, kind, base, after):
                act.wait_ge(pass_done, after)
                if kind == "cross":
                    act.wait_ge(qp_zero, 1)

                def evac_x(w):
                    n = w.n
                    act.wait_ge(C.xT_ps.sem, C.xT_ps.of(n, 1))
                    act.wait_ge(C.proj_ps.sem, C.proj_ps.before(n, C.proj_ps.k))
                    if kind == "local":
                        act.activation(yT[0:64, 0:T], TRP[0:64, 0:T], ACT.Copy)
                        act.activation(yT[64:128, 1:T], TRP[64:128, 0:T - 1], ACT.Copy)\
                           .then_inc(C.yT_sb.sem, 1)
                    else:
                        w = 2 * T if kind == "cross" else T
                        act.activation(yT[:, 0:w], TRP[:, 0:w], ACT.Copy).then_inc(C.yT_sb.sem, 1)

                def square(w, c):
                    n = w.n
                    act.wait_ge(C.proj_ps.sem, C.proj_ps.of(n, c + 1))
                    act.wait_ge(C.norm2.sem, C.norm2.of(n, c - 1) if c >= 2 else C.norm2.before(n, c + 3))
                    act.activation(sq[:, (c % 2) * BANK:(c % 2 + 1) * BANK], PROJ[c % 2][:, :], ACT.Square)\
                       .then_inc(C.squared.sem, 1)

                def store_q(n, p, c, src):
                    act.wait_ge(C.scores.sem, C.scores.before(n, NG, 2))
                    q = QP[:, p * H * T + c * 8 * T:p * H * T + (c + 1) * 8 * T].rearrange(
                        "f (i two t) -> f i two t", two=2, t=T)
                    s = src[:, :].rearrange("f (i t) -> f i t", t=T)
                    act.activation(q[0:64, :, 0, :], s[0:64], ACT.Copy)
                    act.activation(q[64:128, :, 1, :], s[64:128], ACT.Copy).then_inc(C.qk_sb.sem, 1)

                def store_k(n, p, c, src):
                    act.wait_ge(C.scores.sem, C.scores.before(n, NG, 2))
                    act.activation(KT[:, p * 8 * T + c * BANK:p * 8 * T + (c + 1) * BANK], src[:, :], ACT.Copy)\
                       .then_inc(C.qk_sb.sem, 1)

                def store_v(w, c):
                    n, p = w.n, w.p
                    act.wait_ge(C.proj_ps.sem, C.proj_ps.of(n, 4 + c + 1))
                    act.wait_ge(C.av_ps.sem, C.av_ps.before(n, NG, 2))
                    act.activation(V[:, p * H * D + c * BANK:p * H * D + (c + 1) * BANK], PROJ[c % 2][:, :], ACT.Copy)\
                       .then_inc(C.v_sb.sem, 1)

                def store_trans(w, i):
                    n, p = w.n, w.p
                    if kind == "local":
                        act.wait_ge(C.trans_ps.sem, C.trans_ps.of(n, i + 1))
                        src = TRP
                    else:
                        act.wait_ge(C.proj_ps.sem, C.proj_ps.of(n, i + 1))
                        src = PROJ[i % 2]
                    (store_q if i < 2 else store_k)(n, p, i % 2, src)

                def exps(w, g):
                    n, p = w.n, w.p
                    act.wait_ge(C.negmax.sem, C.negmax.of(n, g + 1))
                    act.wait_ge(C.probT_ps.sem, C.probT_ps.before(n, g + 1))
                    act.wait_ge(C.recip.sem, C.recip.before(n, g + 1))
                    for i in range(GH):
                        h = g * GH + i
                        scale = (rn[:, 2 * p * H + h:2 * p * H + h + 1] if kind == "local"
                                 else float((DH if kind == "cross" else DH_SELF) ** -0.5))
                        e = act.activation(P[:, h * T:(h + 1) * T], SPS[g % 2][:, i * T:(i + 1) * T], ACT.Exp,
                                           bias=nb[:, h:h + 1], scale=scale, accum_out=rs[:, h:h + 1])
                    e.then_inc(C.prob.sem, 1)

                def self_k(w):
                    n, p = w.n, w.p
                    act.wait_ge(C.proj_ps.sem, C.proj_ps.of(n, QKV_CHUNKS))
                    act.wait_ge(C.scores.sem, C.scores.before(n, NG, 2))
                    act.activation(KT[:, p * 8 * T:p * 8 * T + T], PROJ[1][:, 0:T], ACT.Copy).then_inc(C.selfk.sem, 1)

                def self_v(w):
                    n, p = w.n, w.p
                    act.wait_ge(C.proj_ps.sem, C.proj_ps.of(n, QKV_CHUNKS))
                    act.wait_ge(C.av_ps.sem, C.av_ps.before(n, NG, 2))
                    act.activation(V[:, p * H * D:(p + 1) * H * D].rearrange("t (h r d) -> t h r d", h=H, d=DH_SELF),
                                   PROJ[1][:, T:T + D].rearrange("t (h d) -> t h d", h=H).unsqueeze(2)
                                   .to_broadcast([T, H, D // DH_SELF, DH_SELF]), ACT.Copy).then_inc(C.selfv.sem, 1)

                def store_pT(w, g):
                    n = w.n
                    act.wait_ge(C.probT_ps.sem, C.probT_ps.of(n, g + 1))
                    act.wait_ge(C.av_ps.sem, C.av_ps.of(n, g - 1) if g >= 2 else C.av_ps.before(n, g + 3))
                    act.activation(PTs[:, (g % 2) * BANK:(g % 2 + 1) * BANK], PTP[:, :], ACT.Copy).then_inc(C.probT.sem, 1)

                def store_o(w, i):
                    n = w.n
                    act.wait_ge(C.av_ps.sem, C.av_ps.of(n, 2 * i + 2))
                    act.wait_ge(C.y_ps.sem, C.y_ps.before(n, 1))
                    act.activation(OT[:, i * BANK:(i + 1) * BANK], OTP[:, :], ACT.Copy).then_inc(C.oT_sb.sem, 1)

                def turn_self(t):
                    t.run(store_pT, 3, 0)
                    t.run(self_v, 2)
                    t.run(store_pT, 3, 1)
                    t.run(exps, 3, 3)
                    t.run(self_k, 1)
                    t.run(store_pT, 3, 2)
                    t.run(exps, 2, 0)
                    t.run(store_pT, 3, 3)
                    t.run(exps, 2, 1)
                    t.run(evac_x, 0)
                    t.run(exps, 2, 2)

                def turn_cross(t):
                    t.run(exps, 3, 2)
                    t.run(store_trans, 2, 3)
                    t.run(store_v, 2, 0)
                    t.run(exps, 3, 3)
                    t.run(evac_x, 1)
                    t.run(store_v, 2, 1)
                    t.run(exps, 2, 0)
                    t.run(store_trans, 1, 0)
                    t.run(exps, 2, 1)
                    t.run(store_o, 3, 0)
                    t.run(store_trans, 1, 1)
                    t.run(store_o, 3, 1)
                    t.run(store_trans, 1, 2)

                def turn_local(t):
                    t.run(exps, 2, 1)
                    t.run(exps, 2, 2)
                    t.run(store_v, 1, 0)
                    t.run(store_trans, 1, 2)
                    t.run(store_v, 1, 1)
                    t.run(store_trans, 1, 3)
                    t.run(evac_x, 0)
                    t.run(exps, 2, 3)
                    t.run(square, 0, 0)
                    t.run(exps, 1, 0)
                    t.run(square, 0, 1)
                    t.run(square, 0, 2)
                    t.run(store_o, 2, 0)
                    t.run(square, 0, 3)
                    t.run(store_trans, 0, 0)
                    t.run(store_trans, 0, 1)
                    t.run(store_o, 2, 1)

                turn_of_kind = {"self": turn_self, "cross": turn_cross, "local": turn_local}[kind]
                pipeline(act, base, turn_of_kind, MAX_LAG[kind])

            def store_xnT(w):
                m = w.n
                act.wait_ge(CF.xnT_ps.sem, CF.xnT_ps.of(m, 1))
                act.wait_ge(CF.up_ps.sem, CF.up_ps.before(m, 3, 2))
                act.activation(xnT[:, w.p * FB * T:(w.p + 1) * FB * T], TRP[:, :], ACT.Identity,
                               bias=WF[:, G_AT + 1:G_AT + 2], scale=WF[:, G_AT:G_AT + 1]).then_inc(CF.xnT.sem, 1)

            def gelu(w, c):
                m, r = w.n, FC[c]
                act.wait_ge(CF.up_ps.sem, CF.up_ps.of(m, c + 1))
                act.wait_ge(CF.gate.sem, CF.gate.before(m, c + 1))
                act.activation(gel[0:r, c * BANK:(c + 1) * BANK], SPS[c % 2][0:r, :], ACT.Gelu,
                               bias=WF[0:r, B1_AT + 3 + c:B1_AT + 4 + c]).then_inc(CF.gelu.sem, 1)

            def turn_ff(t):
                t.run(gelu, 2, 0)
                t.run(gelu, 2, 1)
                t.run(gelu, 2, 2)
                t.run(store_xnT, 1)

            attention(CS, "self", 0, 1)
            attention(CC, "cross", 0, 3)
            act.wait_ge(const_made, 5)
            with act.Fori(0, LAYERS) as l:
                attention(CL, "local", l * UNITS, l * 2 + PASSES_BEFORE_LAYERS)
                act.wait_ge(pass_done, l * 2 + (PASSES_BEFORE_LAYERS + 1))
                act.wait_ge(ffnw_in, l * 16 + 16)
                pipeline(act, l * NFB, turn_ff, MAX_LAG["ff"], NFB)

        @block.vector
        def _(dve):
            give_credit(dve, CS.vector + CC.vector + CL.vector)
            give_credit(dve, CF.vector)
            dve.wait_ge(consts_in, 16 * 6)
            dve.tensor_copy(identb[:, :], ident[:, :])
            dve.tensor_copy(masks[:, :], masks_f[:, :]).then_inc(bf_made, 1)
            dve.wait_ge(x_in, 16)

            def norm_pass(k, src, dst):
                with dve.Fori(0, UNITS // 8) as o:
                    for i in range(8):
                        dve.bn_stats(cols(stats, o * 48 + i * 6, 6), cols(src, o * (8 * D) + i * D, D))\
                           .then_inc(ln_step, 1)
                dve.wait_ge(ln_step, UNITS * (3 * k - 2))
                for u in range(UNITS):
                    dve.bn_aggr(mv[:, 2 * u:2 * u + 2], stats[:, 6 * u:6 * u + 6]).then_inc(ln_step, 1)
                dve.wait_ge(ln_step, UNITS * (3 * k - 1))
                dve.sem_inc(ln_stats, 1)
                dve.wait_ge(ln_rstd, k)
                with dve.Fori(0, UNITS // 8) as o:
                    for i in range(8):
                        dve.tensor_scalar(cols(dst, o * (8 * D) + i * D, D), cols(src, o * (8 * D) + i * D, D),
                                          cols(mv, o * 16 + i * 2, 1), cols(rstd, o * 8 + i, 1),
                                          ALU.subtract, ALU.mult).then_inc(ln_step, 1)
                dve.wait_ge(ln_step, UNITS * 3 * k)
                dve.sem_inc(pass_done, 1)

            def attention(C, kind, base, state):
                def rotate(w, c):
                    n = w.n
                    dve.wait_ge(C.squared.sem, C.squared.of(n, c + 1))
                    dve.wait_ge(C.rsum.sem, C.rsum.of(n, c - 1) if c >= 2 else C.rsum.before(n, c + 3))
                    t = tu[:, (c % 2) * 2 * BANK:(c % 2 + 1) * 2 * BANK].rearrange("t (w h d) -> t w h d", w=2, h=8)
                    ps = PROJ[c % 2][:, :].rearrange("t (h d) -> t h d", h=8).unsqueeze(1).to_broadcast([T, 2, 8, DH])
                    a = (c // 2) * 2 * DH
                    tb = tab[:, a:a + 2 * DH].rearrange("t (w d) -> t w d", w=2).unsqueeze(2).to_broadcast([T, 2, 8, DH])
                    dve.tensor_tensor(t, ps, tb, ALU.mult).then_inc(C.rotated.sem, 1)

                def norm2(w, c):
                    n = w.n
                    dve.wait_ge(C.squared.sem, C.squared.of(n, c + 1))
                    dve.wait_ge(C.seeded.sem, C.seeded.before(n, 2))
                    dve.tensor_reduce(n2[:, c * 8:(c + 1) * 8],
                                      sq[:, (c % 2) * BANK:(c % 2 + 1) * BANK].rearrange("t (h d) -> t h d", h=8),
                                      AX.X, ALU.add).then_inc(C.norm2.sem, 1)

                def seed(w):
                    n = w.n
                    dve.wait_ge(C.norm2.sem, C.norm2.of(n, 4))
                    dve.wait_ge(C.newton.sem, C.newton.before(n, 4 * NEWTON))
                    dve.tensor_scalar(n2c[:, :], n2[:, :], 1e-24, None, ALU.max).then_inc(C.seeded.sem, 1)
                    dve.wait_ge(C.seeded.sem, C.seeded.of(n, 1))
                    dve.tensor_scalar(half_bits[:, :], n2c[:, :].bitcast(I32), 1, None, ALU.arith_shift_right)\
                       .then_inc(C.seeded.sem, 1)
                    dve.tensor_scalar(n2h[:, :], n2c[:, :], -0.5, None, ALU.mult)
                    dve.wait_ge(C.seeded.sem, C.seeded.of(n, 2))
                    dve.tensor_scalar(guess[:, :].bitcast(I32), half_bits[:, :], -1.0, float(MAGIC), ALU.mult, ALU.add)\
                       .then_inc(C.seeded.sem, 1)

                def knorm(w, c):
                    n = w.n
                    dve.wait_ge(C.newton.sem, C.newton.of(n, 4 * NEWTON))
                    dve.wait_ge(C.rsum.sem, C.rsum.of(n, 3 + c))
                    dve.wait_ge(C.trans_ps.sem, C.trans_ps.before(n, 3 + c))
                    dve.tensor_tensor(knb[:, c * BANK:(c + 1) * BANK].rearrange("t (h d) -> t h d", h=8),
                                      rsb[:, (2 + c) * BANK:(3 + c) * BANK].rearrange("t (h d) -> t h d", h=8),
                                      rn[:, (2 * w.p + 1) * H + c * 8:(2 * w.p + 1) * H + (c + 1) * 8].unsqueeze(2).to_broadcast([T, 8, DH]),
                                      ALU.mult).then_inc(C.knorm.sem, 1)

                def rowmax(w, g):
                    n, p = w.n, w.p
                    dve.wait_ge(C.scores.sem, C.scores.of(n, g + 1))
                    a = slice(g * GH, (g + 1) * GH)
                    dve.tensor_reduce(mx[:, a], SPS[g % 2][:, :].rearrange("t (h k) -> t h k", h=GH), AX.X,
                                      ALU.max).then_inc(C.rowmax.sem, 1)
                    dve.wait_ge(C.rowmax.sem, C.rowmax.of(n, g + 1))
                    dve.wait_ge(C.prob.sem, C.prob.before(n, g + 1))
                    if kind == "local":
                        dve.wait_ge(C.newton.sem, C.newton.of(n, 4 * NEWTON))
                        dve.scalar_tensor_tensor(out=nb[:, a], in0=mx[:, a], scalar=-1.0,
                                                 in1=rn[:, 2 * p * H + g * GH:2 * p * H + (g + 1) * GH],
                                                 op0=ALU.mult, op1=ALU.mult).then_inc(C.negmax.sem, 1)
                    else:
                        s = float((DH if kind == "cross" else DH_SELF) ** -0.5)
                        dve.tensor_scalar(nb[:, a], mx[:, a], -s, None, ALU.mult).then_inc(C.negmax.sem, 1)

                def recip(w, g):
                    n = w.n
                    dve.wait_ge(C.prob.sem, C.prob.of(n, g + 1))
                    dve.wait_ge(C.probn.sem, C.probn.before(n, g + 1))
                    a = slice(g * GH, (g + 1) * GH)
                    dve.reciprocal(ri[:, a], rs[:, a]).then_inc(C.recip.sem, 1)

                def store_pT(w, g):
                    n = w.n
                    dve.wait_ge(C.probT_ps.sem, C.probT_ps.of(n, g + 1))
                    dve.wait_ge(C.av_ps.sem, C.av_ps.of(n, g - 1) if g >= 2 else C.av_ps.before(n, g + 3))
                    dve.tensor_copy(PTs[:, (g % 2) * BANK:(g % 2 + 1) * BANK], PTP[:, :]).then_inc(C.probT.sem, 1)

                def self_q(w):
                    n, p = w.n, w.p
                    dve.wait_ge(C.proj_ps.sem, C.proj_ps.of(n, QKV_CHUNKS))
                    dve.wait_ge(C.scores.sem, C.scores.before(n, NG, 2))
                    dve.tensor_tensor(QP[:, p * H * T:(p + 1) * H * T].rearrange("f (h t) -> f h t", h=H),
                                      PROJ[0][:, 0:T].unsqueeze(1).to_broadcast([128, H, T]),
                                      headmask[:, :].unsqueeze(2).to_broadcast([128, H, T]), ALU.mult)\
                       .then_inc(C.selfq.sem, 1)

                def pick(w, g):
                    n = w.n
                    dve.wait_ge(C.av_ps.sem, C.av_ps.of(n, g + 1))
                    s = sq[:, (g % 2) * BANK:(g % 2 + 1) * BANK]
                    dve.tensor_tensor(s.rearrange("f (a r) -> f a r", r=D // DH_SELF),
                                      OTP[:, :].rearrange("f (a r) -> f a r", r=D // DH_SELF),
                                      headmask[:, :].unsqueeze(1).to_broadcast([128, BANK // H, H]), ALU.mult)\
                       .then_inc(C.picked.sem, 1)
                    dve.wait_ge(C.picked.sem, C.picked.of(n, g + 1))
                    dve.wait_ge(C.y_ps.sem, C.y_ps.before(n, 1))
                    w = BANK // H
                    dve.tensor_reduce(OT[:, g * w:(g + 1) * w], s.rearrange("f (a r) -> f a r", r=D // DH_SELF),
                                      AX.X, ALU.add).then_inc(C.selfo.sem, 1)

                def update(w):
                    n, u = w.n, w.u
                    dve.wait_ge(C.y_ps.sem, C.y_ps.of(n, 1))
                    dve.tensor_tensor(cols(state, u * D, D), cols(state, u * D, D), YPS[:, 0:D], ALU.add)\
                       .then_inc(C.updated.sem, 1)

                def turn_self(t):
                    t.run(recip, 3, 3)
                    t.run(pick, 3, 1)
                    t.run(rowmax, 2, 1)
                    t.run(pick, 3, 2)
                    t.run(rowmax, 2, 2)
                    t.run(recip, 2, 0)
                    t.run(pick, 3, 3)
                    t.run(recip, 2, 1)
                    t.run(self_q, 1)
                    t.run(rowmax, 2, 3)
                    t.run(recip, 2, 2)
                    t.run(pick, 2, 0)
                    t.run(rowmax, 1, 0)
                    t.run(update, 3)

                def turn_cross(t):
                    t.run(recip, 2, 0)
                    t.run(rowmax, 2, 2)
                    t.run(store_pT, 3, 3)
                    t.run(store_pT, 2, 0)
                    t.run(recip, 2, 1)
                    t.run(rowmax, 2, 3)
                    t.run(recip, 2, 2)
                    t.run(rowmax, 1, 0)
                    t.run(store_pT, 2, 1)
                    t.run(rowmax, 1, 1)
                    t.run(store_pT, 2, 2)
                    t.run(update, 3)
                    t.run(recip, 2, 3)

                def turn_local(t):
                    t.run(knorm, 1, 1)
                    t.run(recip, 2, 2)
                    t.run(rowmax, 2, 3)
                    t.run(store_pT, 2, 1)
                    t.run(rowmax, 1, 0)
                    t.run(store_pT, 2, 2)
                    t.run(recip, 2, 3)
                    t.run(rotate, 0, 0)
                    t.run(norm2, 0, 0)
                    t.run(recip, 1, 0)
                    t.run(rotate, 0, 1)
                    t.run(norm2, 0, 1)
                    t.run(rotate, 0, 2)
                    t.run(norm2, 0, 2)
                    t.run(norm2, 0, 3)
                    t.run(seed, 0)
                    t.run(store_pT, 2, 3)
                    t.run(rowmax, 1, 1)
                    t.run(rowmax, 1, 2)
                    t.run(rotate, 0, 3)
                    t.run(update, 2)
                    t.run(recip, 1, 1)
                    t.run(knorm, 0, 0)
                    t.run(store_pT, 1, 0)

                turn_of_kind = {"self": turn_self, "cross": turn_cross, "local": turn_local}[kind]
                pipeline(dve, base, turn_of_kind, MAX_LAG[kind])
                dve.wait_ge(C.updated.sem, C.updated.of(base + (UNITS - 1), 1))
                dve.sem_inc(pass_done, 1)

            def block_of(w):
                return cols(XB, w.u * (FB * D), FB * D)

            def statistics(w):
                m = w.n
                dve.wait_ge(CF.shift_ps.sem, CF.shift_ps.of(m, 1))
                dve.wait_ge(CF.rstd.sem, CF.rstd.before(m, 1))
                dve.wait_ge(CF.cent.sem, CF.cent.before(m, 1))
                st = stats[:, 0:FB * 12].rearrange("t (u s) -> t u s", s=12)
                for u in range(FB):
                    dve.bn_stats(st[:, u, 0:6], cols(XB, w.u * (FB * D) + u * D, 64))
                    b = dve.bn_stats(st[:, u, 6:12], YPS[:, u * 64:(u + 1) * 64])
                b.then_inc(CF.bn1.sem, 1)
                dve.wait_ge(CF.bn1.sem, CF.bn1.of(m, 1))
                hold(dve)
                for u in range(FB):
                    b = dve.bn_aggr(mv[:, 2 * u:2 * u + 2], st[:, u, :])
                b.then_inc(CF.bn2.sem, 1)

            def center(w):
                m = w.n
                dve.wait_ge(CF.bn2.sem, CF.bn2.of(m, 1))
                dve.wait_ge(CF.xn.sem, CF.xn.before(m, 1))
                blk = block_of(w).rearrange("t (u d) -> t u d", u=FB)
                mean = mv[:, 0:2 * FB].rearrange("t (u two) -> t u two", two=2)[:, :, 0:1].to_broadcast([T, FB, 64])
                xcv = xc[:, :].rearrange("t (u d) -> t u d", u=FB)
                dve.tensor_tensor(xcv[:, :, 0:64], blk[:, :, 0:64], mean, ALU.subtract)
                dve.tensor_tensor(xcv[:, :, 64:128], YPS[:, 0:FB * 64].rearrange("t (u d) -> t u d", u=FB), mean,
                                  ALU.subtract).then_inc(CF.cent.sem, 1)

            def make_xn(w):
                m = w.n
                dve.wait_ge(CF.cent.sem, CF.cent.of(m, 1))
                dve.wait_ge(CF.rstd.sem, CF.rstd.of(m, 1))
                dve.wait_ge(CF.xnT_ps.sem, CF.xnT_ps.before(m, 1))
                dve.tensor_tensor(xn[:, :].rearrange("t (u d) -> t u d", u=FB),
                                  xc[:, :].rearrange("t (u d) -> t u d", u=FB),
                                  rstd[:, 0:FB].unsqueeze(2).to_broadcast([T, FB, D]), ALU.mult).then_inc(CF.xn.sem, 1)

            def gate(w, c):
                m, r = w.n, FC[c]
                dve.wait_ge(CF.gelu.sem, CF.gelu.of(m, c + 1))
                dve.wait_ge(CF.down_ps.sem, CF.down_ps.before(m, 1))
                a = slice(c * BANK, (c + 1) * BANK)
                dve.scalar_tensor_tensor(out=gT[0:r, a], in0=PROJ[c % 2][0:r, :],
                                         scalar=WF[0:r, B1_AT + c:B1_AT + c + 1], in1=gel[0:r, a],
                                         op0=ALU.add, op1=ALU.mult).then_inc(CF.gate.sem, 1)

            def ff_update(w):
                m = w.n
                dve.wait_ge(CF.down_ps.sem, CF.down_ps.of(m, 1))
                dve.tensor_tensor(block_of(w), block_of(w), PTP[:, :], ALU.add).then_inc(CF.upd.sem, 1)

            def turn_ff(t):
                t.run(statistics, 0)
                t.run(center, 0)
                t.run(ff_update, 2)
                t.run(gate, 1, 0)
                t.run(make_xn, 0)
                t.run(gate, 1, 1)
                t.run(gate, 1, 2)

            norm_pass(1, XA, XB)
            attention(CS, "self", 0, XA)
            norm_pass(2, XA, XB)
            attention(CC, "cross", 0, XA)
            norm_pass(3, XA, XB)
            with dve.Fori(0, LAYERS) as l:
                dve.tensor_tensor(tab[:, :].rearrange("t (w s d) -> t w s d", w=2, s=2),
                                  rot[:, :].rearrange("t (w s d) -> t w s d", w=2, s=2),
                                  cols(scl, l * (2 * DH), 2 * DH).rearrange("t (w d) -> t w d", w=2).unsqueeze(2)
                                  .to_broadcast([T, 2, 2, DH]), ALU.mult).then_inc(tab_made, 1)
                dve.wait_ge(tab_made, l + 1)
                attention(CL, "local", l * UNITS, XB)
                dve.wait_ge(ffnw_in, l * 16 + 16)
                hold(dve)
                pipeline(dve, l * NFB, turn_ff, MAX_LAG["ff"], NFB)
                dve.wait_ge(CF.upd.sem, CF.upd.of(l * NFB + (NFB - 1), 1))
                dve.sem_inc(pass_done, 1)
            dve.tensor_tensor(XA[:, :], XA[:, :], XB[:, :], ALU.add).then_inc(pass_done, 1)

        @block.tensor
        def _(pe):
            give_credit(pe, CS.tensor + CC.tensor + CL.tensor)
            give_credit(pe, CF.tensor)
            pe.wait_ge(consts_in, 16 * 6)
            pe.wait_ge(const_made, 4)
            pe.wait_ge(bf_made, 1)

            def attention(C, kind, base, after):
                pe.wait_ge(pass_done, after)

                def transpose_x(w):
                    n = w.n
                    pe.wait_ge(C.staged.sem, C.staged.of(n, 1))
                    if kind == "local":
                        pe.wait_ge(C.qk_sb.sem, C.qk_sb.before(n, 4))
                    else:
                        pe.wait_ge(C.yT_sb.sem, C.yT_sb.before(n, 1))
                    i = pe.transpose(TRP[:, 0:T], xa[:, 0:D], ident[:, :])
                    if kind == "cross":
                        i = pe.transpose(TRP[:, T:2 * T], xa[:, D:2 * D], ident[:, :])
                    i.then_inc(C.xT_ps.sem, 1)

                def project_self(w):
                    n = w.n
                    pe.wait_ge(C.yT_sb.sem, C.yT_sb.of(n, 1))
                    pe.wait_ge(C.selfq.sem, C.selfq.before(n, 1))
                    pe.wait_ge(C.selfv.sem, C.selfv.before(n, 1))
                    pe.wait_ge(C.selfk.sem, C.selfk.before(n, 1))
                    pe.matmul(PROJ[0][:, 0:T], WF[:, 0:D], yT[:, 0:T], start=True, stop=True)
                    pe.matmul(PROJ[1][:, T:T + D], yT[:, 0:T], WF[:, 2 * D:3 * D], start=True, stop=True)
                    pe.matmul(PROJ[1][:, 0:T], WF[:, D:2 * D], yT[:, 0:T], start=True, stop=True)\
                      .then_inc(C.proj_ps.sem, QKV_CHUNKS)

                def project(w, c):
                    n = w.n
                    if c == 0:
                        pe.wait_ge(C.yT_sb.sem, C.yT_sb.of(n, 1))
                    if c < 2:
                        pe.wait_ge(C.v_sb.sem, C.v_sb.before(n, c + 1))
                    elif kind == "local":
                        pe.wait_ge(C.rotated.sem, C.rotated.of(n, c - 1))
                    else:
                        pe.wait_ge(C.qk_sb.sem, C.qk_sb.of(n, c - 1))
                    if kind == "local" or c >= 4:
                        a = T if kind == "cross" else 0
                        pe.matmul(PROJ[c % 2][:, :], yT[:, a:a + T], W[:, c * BANK:(c + 1) * BANK],
                                  start=True, stop=True).then_inc(C.proj_ps.sem, 1)
                        return
                    a = T if c >= 2 else 0
                    for i in range(4):
                        o = c * BANK + i * 128
                        mm = pe.matmul(PROJ[c % 2][:, i * T:(i + 1) * T], W[:, o:o + 128], yT[:, a:a + T],
                                       start=True, stop=True)
                    mm.then_inc(C.proj_ps.sem, 1)

                def transpose_qk(w, i):
                    n = w.n
                    if i < 2:
                        pe.wait_ge(C.rsum.sem, C.rsum.of(n, i + 1))
                    else:
                        pe.wait_ge(C.knorm.sem, C.knorm.of(n, i - 1))
                    if i == 0:
                        pe.wait_ge(C.yT_sb.sem, C.yT_sb.of(n, 1))
                    else:
                        pe.wait_ge(C.qk_sb.sem, C.qk_sb.of(n, i))
                    src = rsb[:, i * BANK:(i + 1) * BANK] if i < 2 else knb[:, (i - 2) * BANK:(i - 1) * BANK]
                    for j in range(4):
                        t = pe.transpose(TRP[:, j * T:(j + 1) * T], src[:, j * 128:(j + 1) * 128], ident[:, :])
                    t.then_inc(C.trans_ps.sem, 1)

                def scores(w, g):
                    n, p = w.n, w.p
                    if g == 0 and kind == "local":
                        pe.wait_ge(C.qk_sb.sem, C.qk_sb.of(n, 4))
                    elif g == 0 and kind == "self":
                        pe.wait_ge(C.selfq.sem, C.selfq.of(n, 1))
                        pe.wait_ge(C.selfk.sem, C.selfk.of(n, 1))
                    elif g == 0:
                        pe.wait_ge(C.qk_sb.sem, C.qk_sb.of(n, 4))
                    pe.wait_ge(C.prob.sem, C.prob.of(n, g - 1) if g >= 2 else C.prob.before(n, g + 3))
                    bank = SPS[g % 2]
                    masked = kind != "cross"
                    if masked:
                        a = 0 if kind == "self" else T
                        pe.matmul(bank[:, :].rearrange("t (h k) -> t h k", h=GH), identb[:, :],
                                  masks[:, a:a + T].unsqueeze(1).to_broadcast([128, GH, T]), start=True, stop=False)
                    for i in range(GH):
                        h = g * GH + i
                        c = 0 if kind == "self" else h // 2
                        mm = pe.matmul(bank[:, i * T:(i + 1) * T], QP[:, (p * H + h) * T:(p * H + h + 1) * T],
                                       KT[:, (p * 8 + c) * T:(p * 8 + c + 1) * T],
                                       start=not masked, stop=(not masked or i == GH - 1))
                    mm.then_inc(C.scores.sem, 1)

                def transpose_p(w, g):
                    n = w.n
                    pe.wait_ge(C.probn.sem, C.probn.of(n, g + 1))
                    pe.wait_ge(C.probT.sem, C.probT.of(n, g) if g else C.probT.before(n, NG))
                    for i in range(GH):
                        h = g * GH + i
                        t = pe.transpose(PTP[:, i * T:(i + 1) * T], P[:, h * T:(h + 1) * T], ident[:, :])
                    t.then_inc(C.probT_ps.sem, 1)

                def weigh_v(w, g):
                    n, p = w.n, w.p
                    pe.wait_ge(C.probT.sem, C.probT.of(n, g + 1))
                    if kind == "self":
                        if g == 0:
                            pe.wait_ge(C.selfv.sem, C.selfv.of(n, 1))
                        pe.wait_ge(C.picked.sem, C.picked.of(n, g) if g else C.picked.before(n, NG))
                    elif g % 2 == 0:
                        pe.wait_ge(C.v_sb.sem, C.v_sb.of(n, g // 2 + 1))
                        pe.wait_ge(C.oT_sb.sem, C.oT_sb.of(n, 1) if g else C.oT_sb.before(n, 2))
                    for i in range(GH):
                        h = g * GH + i
                        pt = PTs[:, (g % 2) * BANK + i * T:(g % 2) * BANK + (i + 1) * T]
                        if kind == "self":
                            mm = pe.matmul(OTP[:, i * T:(i + 1) * T], V[:, (p * H + h) * D:(p * H + h + 1) * D],
                                           pt, start=True, stop=True)
                        else:
                            r, c = (h % 2) * 64, (h % 8) // 2
                            v0 = p * H * D + h * DH
                            mm = pe.matmul(OTP[r:r + 64, c * T:(c + 1) * T], V[:, v0:v0 + DH], pt,
                                           start=True, stop=True)
                    mm.then_inc(C.av_ps.sem, 1)

                def project_out(w):
                    n = w.n
                    if kind == "self":
                        pe.wait_ge(C.selfo.sem, C.selfo.of(n, NG))
                    else:
                        pe.wait_ge(C.oT_sb.sem, C.oT_sb.of(n, 2))
                    pe.wait_ge(C.updated.sem, C.updated.before(n, 1))
                    if kind == "self":
                        pe.matmul(YPS[:, 0:D], ones[:, :], BO[:, :], start=True, stop=False)
                        pe.matmul(YPS[:, 0:D], OT[:, 0:T], WF[:, 3 * D:4 * D], start=False, stop=True)\
                          .then_inc(C.y_ps.sem, 1)
                        return
                    for c in range(8):
                        mm = pe.matmul(YPS[:, 0:D], OT[:, c * T:(c + 1) * T], W[:, WO_AT + c * D:WO_AT + (c + 1) * D],
                                       start=c == 0, stop=c == 7)
                    mm.then_inc(C.y_ps.sem, 1)

                def turn_self(t):
                    t.run(weigh_v, 3, 1)
                    t.run(transpose_p, 3, 2)
                    t.run(scores, 2, 1)
                    t.run(weigh_v, 3, 2)
                    t.run(transpose_p, 3, 3)
                    t.run(scores, 2, 2)
                    t.run(transpose_x, 0)
                    t.run(weigh_v, 3, 3)
                    t.run(scores, 2, 3)
                    t.run(transpose_p, 2, 0)
                    t.run(project_out, 3)
                    t.run(weigh_v, 2, 0)
                    t.run(transpose_p, 2, 1)
                    t.run(scores, 1, 0)
                    t.run(project_self, 0)

                def turn_cross(t):
                    t.run(transpose_p, 3, 1)
                    t.run(scores, 2, 0)
                    t.run(weigh_v, 3, 0)
                    t.run(project, 2, 5)
                    t.run(scores, 2, 1)
                    t.run(project, 1, 0)
                    t.run(transpose_x, 0)
                    t.run(transpose_p, 3, 2)
                    t.run(weigh_v, 3, 1)
                    t.run(project, 1, 1)
                    t.run(scores, 2, 2)
                    t.run(project, 1, 2)
                    t.run(transpose_p, 3, 3)
                    t.run(scores, 2, 3)
                    t.run(weigh_v, 3, 2)
                    t.run(weigh_v, 3, 3)
                    t.run(transpose_p, 2, 0)
                    t.run(project, 1, 3)
                    t.run(project_out, 3)
                    t.run(project, 1, 4)

                def turn_local(t):
                    t.run(scores, 2, 3)
                    t.run(transpose_qk, 1, 2)
                    t.run(project, 1, 5)
                    t.run(transpose_qk, 1, 3)
                    t.run(transpose_p, 2, 1)
                    t.run(weigh_v, 2, 0)
                    t.run(transpose_x, 0)
                    t.run(scores, 1, 0)
                    t.run(project, 0, 0)
                    t.run(transpose_p, 2, 2)
                    t.run(project, 0, 1)
                    t.run(scores, 1, 1)
                    t.run(project, 0, 2)
                    t.run(weigh_v, 2, 1)
                    t.run(transpose_qk, 0, 0)
                    t.run(project, 0, 3)
                    t.run(scores, 1, 2)
                    t.run(transpose_p, 2, 3)
                    t.run(weigh_v, 2, 2)
                    t.run(transpose_qk, 0, 1)
                    t.run(weigh_v, 2, 3)
                    t.run(project, 0, 4)
                    t.run(project_out, 2)
                    t.run(transpose_p, 1, 0)

                turn_of_kind = {"self": turn_self, "cross": turn_cross, "local": turn_local}[kind]
                pipeline(pe, base, turn_of_kind, MAX_LAG[kind])

            def shift_state(w):
                m = w.n
                pe.wait_ge(CF.cent.sem, CF.cent.before(m, 1))
                blk = cols(XB, w.u * (FB * D), FB * D).rearrange("t (u d) -> t u d", u=FB)
                pe.matmul(YPS[:, 0:FB * 64].rearrange("t (u d) -> t u d", u=FB), shift[:, :], blk[:, :, 64:128],
                          start=True, stop=True).then_inc(CF.shift_ps.sem, 1)

            def transpose_xn(w):
                m = w.n
                pe.wait_ge(CF.xn.sem, CF.xn.of(m, 1))
                pe.wait_ge(CF.xnT.sem, CF.xnT.before(m, 1))
                for u in range(FB):
                    t = pe.transpose(TRP[:, u * T:(u + 1) * T], xn[:, u * D:(u + 1) * D], ident[:, :])
                t.then_inc(CF.xnT_ps.sem, 1)

            def up(w, c):
                m, r = w.n, FC[c]
                if c == 0:
                    pe.wait_ge(CF.xnT.sem, CF.xnT.of(m, 1))
                pe.wait_ge(CF.gate.sem, CF.gate.of(m, 1) if c == 2 else CF.gate.before(m, [3, 2][c]))
                x = xnT[:, w.p * FB * T:(w.p + 1) * FB * T]
                pe.matmul(SPS[c % 2][0:r, :], WF[:, FF + c * 128:FF + c * 128 + r], x, start=True, stop=True)
                pe.matmul(PROJ[c % 2][0:r, :], WF[:, c * 128:c * 128 + r], x, start=True, stop=True)\
                  .then_inc(CF.up_ps.sem, 1)

            def down(w):
                m = w.n
                pe.wait_ge(CF.gate.sem, CF.gate.of(m, 3))
                pe.wait_ge(CF.upd.sem, CF.upd.before(m, 1))
                pe.matmul(PTP[:, :].rearrange("t (u d) -> t u d", u=FB), ones[:, :],
                          WF[0:1, B2_AT:B2_AT + D].unsqueeze(1).to_broadcast([1, FB, D]), start=True, stop=False)
                for u in range(FB):
                    for c, r in enumerate(FC):
                        mm = pe.matmul(PTP[:, u * D:(u + 1) * D], gT[0:r, c * BANK + u * T:c * BANK + (u + 1) * T],
                                       WF[0:r, W2_AT + c * D:W2_AT + (c + 1) * D], start=False,
                                       stop=(u == FB - 1 and c == 2))
                mm.then_inc(CF.down_ps.sem, 1)

            def turn_ff(t):
                t.run(up, 2, 1)
                t.run(up, 2, 2)
                t.run(transpose_xn, 1)
                t.run(shift_state, 0)
                t.run(up, 1, 0)
                t.run(down, 2)

            pe.wait_ge(selfw_in, 32)
            attention(CS, "self", 0, 1)
            pe.wait_ge(attnw_in, 16)
            attention(CC, "cross", 0, 3)
            with pe.Fori(0, LAYERS) as l:
                pe.wait_ge(attnw_in, l * 16 + 32)
                attention(CL, "local", l * UNITS, l * 2 + PASSES_BEFORE_LAYERS)
                pe.wait_ge(pass_done, l * 2 + (PASSES_BEFORE_LAYERS + 1))
                pe.wait_ge(ffnw_in, l * 16 + 16)
                hold(pe)
                pipeline(pe, l * NFB, turn_ff, MAX_LAG["ff"], NFB)


def constants():
    import numpy as np
    f = np.float32
    half = np.arange(0, DH, 2, dtype=f)
    inv_freq = f(1.0) / f(10000.0) ** (half / f(DH))
    t = np.arange(T, dtype=f)
    freqs = t[:, None] * inv_freq[None, :]
    base = (half + f(0.4 * DH)) / f(1.4 * DH)
    power = (t - T // 2) / f(16)
    scale = base[None, :] ** power[:, None]
    cos, sin = np.cos(freqs), np.sin(freqs)
    parts = []
    for s in (scale * f(QK_SCALE), f(1.0) / scale):
        parts += [cos * s, cos * s, sin * s, -sin * s]
    rot = np.concatenate(parts, 1).astype(f)
    ident = np.eye(128, dtype=f)
    shift = np.eye(128, k=1, dtype=f)
    i, j = np.arange(T)[:, None], np.arange(T)[None, :]
    far = f(-1e30)
    causal = np.where(j > i, far, f(0))
    band = np.where((j > i) | (i - j > 32), far, f(0))
    masks = np.concatenate([causal, band], 1).astype(f)
    head = np.arange(D) // DH_SELF
    headmask = (head[:, None] == np.arange(H)[None, :]).astype(f)
    return ident, shift, rot, headmask, masks


def kernel(x, ctx_1024, L0_attn_Wq, L0_attn_Wk, L0_attn_Wv, L0_attn_Wo, L0_attn_bo, L0_xattn_Wq, L0_xattn_Wk,
           L0_xattn_Wv, L0_xattn_Wo, L0_ffn_Wqkv, L0_ffn_q_scale, L0_ffn_k_scale, L0_ffn_Wo, L0_ffn_ln_g,
           L0_ffn_ln_b, L0_ffn_W1, L0_ffn_b1, L0_ffn_W2, L0_ffn_b2):
    import numpy as np
    import concourse.bacc as bacc
    from concourse.bass_utils import run_bass_kernel_spmd

    def rows(w):
        w = np.asarray(w)
        return w.reshape(-1, 128, w.shape[-1]).transpose(1, 0, 2).reshape(128, -1)

    A = np.asarray
    self_w = np.concatenate([A(L0_attn_Wq), A(L0_attn_Wk), A(L0_attn_Wv), A(L0_attn_Wo)], 1)
    cross_w = np.concatenate([A(L0_xattn_Wq), A(L0_xattn_Wk), A(L0_xattn_Wv), rows(L0_xattn_Wo)], 1)
    attn_w = np.stack([np.concatenate([A(L0_ffn_Wqkv)[l], rows(A(L0_ffn_Wo)[l])], 1) for l in range(LAYERS)])
    qk_scale = np.concatenate([A(L0_ffn_q_scale), A(L0_ffn_k_scale)], 1).reshape(1, -1)
    ffn_w = np.zeros((LAYERS, 128, FFN_COLS), A(L0_ffn_W1).dtype)
    for l in range(LAYERS):
        ffn_w[l, :, 0:2 * FF] = A(L0_ffn_W1)[l]
        for c, w in enumerate(FC):
            ffn_w[l, 0:w, W2_AT + c * D:W2_AT + (c + 1) * D] = A(L0_ffn_W2)[l, c * 128:c * 128 + w]
            ffn_w[l, 0:w, B1_AT + c] = A(L0_ffn_b1)[l, c * 128:c * 128 + w]
            ffn_w[l, 0:w, B1_AT + 3 + c] = A(L0_ffn_b1)[l, FF + c * 128:FF + c * 128 + w]
        ffn_w[l, :, G_AT] = A(L0_ffn_ln_g)[l]
        ffn_w[l, :, G_AT + 1] = A(L0_ffn_ln_b)[l]
        ffn_w[l, 0, B2_AT:B2_AT + D] = A(L0_ffn_b2)[l]
    ident, shift, rot, headmask, masks = constants()
    arrays = {
        "x": x, "ctx": ctx_1024, "self_w": self_w, "self_bo": A(L0_attn_bo).reshape(1, D), "cross_w": cross_w,
        "attn_w": attn_w, "qk_scale": qk_scale, "ffn_w": ffn_w, "ident": ident, "shift": shift, "rot": rot,
        "headmask": headmask, "masks": masks,
    }
    nc = bacc.Bacc("TRN2", target_bir_lowering=False, num_devices=1)
    feeds, args = {}, []
    for name, a in arrays.items():
        a = np.ascontiguousarray(a)
        feeds[f"{name}_dram"] = a
        args.append(nc.dram_tensor(f"{name}_dram", a.shape, mybir.dt.from_np(a.dtype), kind="ExternalInput").ap())
    args.append(nc.dram_tensor("out_dram", (UNITS, T, D), FP32, kind="ExternalOutput").ap())
    build(nc, *args)
    r = run_bass_kernel_spmd(nc, [feeds], core_ids=[0])
    return r.results[0]["out_dram"]
```

```python
import concourse.bass as bass
from concourse import mybir
from contextlib import ExitStack

FP32 = mybir.dt.float32
BF16 = mybir.dt.bfloat16
FP32R = mybir.dt.float32r
I32 = mybir.dt.int32
ALU = mybir.AluOpType
ACT = mybir.ActivationFunctionType
AX = mybir.AxisListType

UNITS = 32
T = 128
D = 128
H = 16
GH = 4
NG = H // GH
DH = 64
INNER = H * DH
DH_SELF = D // H
QK_SCALE = 8
LAYERS = 6
FF = 341
FC = [128, 128, FF - 256]
FFP = len(FC) * 128
BANK = 512
QKV = 3 * INNER
QKV_CHUNKS = 3 * INNER // BANK
FB = 4
NFB = UNITS // FB
EPS = 1e-5
CREDIT = 2
MAX_LAG = {"self": 4, "cross": 4, "local": 4, "ff": 2}
NU = 8
NEWTON = 3
MAGIC = 0x5F3759DF

WO_AT = 3 * INNER
ATTN_COLS = WO_AT + (INNER // 128) * D
W2_AT = 2 * FFP
B1_AT = W2_AT + 3 * D
G_AT = B1_AT + 6
B2_AT = G_AT + 2
FFN_COLS = B2_AT + D


class Counter:

    def __init__(self, sem, per_unit):
        self.sem, self.k = sem, per_unit

    def of(self, n, step):
        return (n + CREDIT) * self.k + step

    def before(self, n, step, back=1):
        return (n + (CREDIT - back)) * self.k + step


def build(nc, x, ctx_in, self_w, self_bo, cross_w, attn_w, qk_scale, ffn_w, ident_in, shift_in,
          rot_in, headmask_in, masks_in, out):
    stack = ExitStack()
    with stack:
        def sb(name, shape, dt=FP32):
            return stack.enter_context(nc.sbuf_tensor(name, shape, dt))

        def sem(name):
            return stack.enter_context(nc.semaphore(name))

        XA = sb("XA", [T, UNITS * D])
        XB = sb("XB", [T, UNITS * D])
        BO = sb("BO", [1, D])
        ident = sb("ident", [128, 128])
        shift = sb("shift", [128, 128])
        identb = sb("identb", [128, 128], BF16)
        masks = sb("masks", [128, 2 * T], BF16)
        masks_f = sb("masks_f", [128, 2 * T])
        headmask = sb("headmask", [128, H])
        rot = sb("rot", [T, 4 * DH])
        scl = sb("scl", [T, LAYERS * 2 * DH])
        tab = sb("tab", [T, 4 * DH])
        ones = sb("ones", [1, 128])
        powc = sb("powc", [T, 32])
        three_halves = sb("three_halves", [T, 2 * H])
        xa = sb("xa", [T, 2 * D])
        yT = sb("yT", [D, 2 * T])
        yTh = sb("yTh", [D, T], FP32R)
        yTl = sb("yTl", [D, T], FP32R)
        sq = sb("sq", [T, 2 * BANK])
        n2 = sb("n2", [T, 2 * H])
        n2c = sb("n2c", [T, 2 * H])
        n2h = sb("n2h", [T, 2 * H])
        half_bits = sb("half_bits", [T, 2 * H], I32)
        guess = sb("guess", [T, 2 * H])
        newt = sb("newt", [T, 2 * H])
        rn = sb("rn", [T, 2 * 2 * H])
        rsb = sb("rsb", [T, 2 * INNER])
        knb = sb("knb", [T, INNER])
        QP = sb("QP", [128, 2 * H * T])
        KT = sb("KT", [128, 2 * 8 * T])
        V = sb("V", [T, 2 * H * D])
        P = sb("P", [T, H * T])
        mx = sb("mx", [T, H])
        nb = sb("nb", [T, H])
        rs = sb("rs", [T, H])
        ri = sb("ri", [T, H])
        PTs = sb("PTs", [T, 2 * BANK])
        OT = sb("OT", [128, 8 * T])
        stats = sb("stats", [T, UNITS * 6])
        mv = sb("mv", [T, UNITS * 2])
        rstd = sb("rstd", [T, UNITS])
        xc = sb("xc", [T, FB * D])
        xn = sb("xn", [T, FB * D])
        xnT = sb("xnT", [D, 2 * FB * T])
        gel = sb("gel", [128, 3 * BANK])
        gT = sb("gT", [128, 3 * BANK])
        with ExitStack() as first:
            def early(name, shape):
                return first.enter_context(nc.sbuf_tensor(name, shape, FP32))

            W = early("W", [128, ATTN_COLS])
            WF = early("WF", [128, FFN_COLS])
            CTX = early("CTX", [T, UNITS * D])
            tu = early("tu", [T, 2 * 2 * BANK])
        W_low = sb("W_low", [128, ATTN_COLS], FP32R)
        WF_low = sb("WF_low", [128, FFN_COLS], FP32R)
        W_high = sb("W_high", [128, QKV], FP32R)
        WF_high = sb("WF_high", [128, UNITS * D - QKV], FP32R)
        xnT_high = sb("xnT_high", [D, 2 * FB * T], FP32R)
        xnT_low = sb("xnT_low", [D, 2 * FB * T], FP32R)

        banks = [stack.enter_context(nc.psum_tensor(f"bank{i}", [128, BANK], FP32)) for i in range(8)]
        PROJ = banks[0:2]
        TRP, YPS = banks[2], banks[3]
        SPS = banks[4:6]
        PTP, OTP = banks[6], banks[7]
        GATES = [SPS[0], SPS[1], OTP]
        XTP = YPS[:, 0:T]
        RESULT = {"self": YPS[:, 0:D], "cross": OTP[:, 0:D], "local": OTP[:, 0:D]}

        consts_in = sem("consts_in")
        x_in = [sem(f"x_in{o}") for o in range(UNITS // NU)]
        ctx_sem = sem("ctx_in")
        selfw_in = sem("selfw_in")
        attnw_in = sem("attnw_in")
        ffnw_in = sem("ffnw_in")
        out_sem = sem("out_sem")
        const_made = sem("const_made")
        bf_made = sem("bf_made")
        held = sem("held")
        pass_done = sem("pass_done")
        ln_step = sem("ln_step")
        ln_stats = sem("ln_stats")
        ln_eps = sem("ln_eps")
        ln_rstd = sem("ln_rstd")
        tab_made = sem("tab_made")
        qp_zero = sem("qp_zero")
        ffnw_high = sem("ffnw_high")
        attnw_high = sem("attnw_high")
        attnw_split = sem("attnw_split")
        ffnw_split = sem("ffnw_split")

        class Counters:

            def __init__(self, kind):
                def c(what, per_unit=1):
                    return Counter(sem(f"{kind}_{what}"), per_unit)

                local, alone = kind == "local", kind == "self"
                self.xT_ps, self.proj_ps = c("xT_ps"), c("proj_ps", QKV_CHUNKS)
                self.scores, self.probT_ps = c("scores", NG), c("probT_ps", NG)
                self.av_ps, self.y_ps = c("av_ps", NG), c("y_ps")
                self.tensor = [self.xT_ps, self.proj_ps, self.scores, self.probT_ps, self.av_ps, self.y_ps]
                self.yT_sb, self.prob = c("yT_sb"), c("prob", NG)
                self.scalar = [self.yT_sb, self.prob]
                self.rowmax, self.negmax = c("rowmax", NG), c("negmax", NG)
                self.recip, self.updated = c("recip", NG), c("updated")
                self.vector = [self.rowmax, self.negmax, self.recip, self.updated]
                self.staged, self.probn = c("staged"), c("probn", NG)
                self.pool = [self.staged, self.probn]
                self.probT = c("probT", NG)
                (self.scalar if alone else self.vector).append(self.probT)
                if alone:
                    self.selfk, self.selfv = c("selfk"), c("selfv")
                    self.scalar += [self.selfk, self.selfv]
                    self.selfq, self.picked, self.selfo = c("selfq"), c("picked", NG), c("selfo", NG)
                    self.vector += [self.selfq, self.picked, self.selfo]
                else:
                    self.qk_sb, self.v_sb, self.oT_sb = c("qk_sb", 4), c("v_sb", 2), c("oT_sb", 2)
                    self.scalar += [self.qk_sb, self.v_sb, self.oT_sb]
                if local:
                    self.trans_ps = c("trans_ps", 4)
                    self.tensor.append(self.trans_ps)
                    self.squared = c("squared", 4)
                    self.scalar.append(self.squared)
                    self.rotated, self.norm2 = c("rotated", 4), c("norm2", 4)
                    self.seeded, self.knorm = c("seeded", 3), c("knorm", 2)
                    self.vector += [self.rotated, self.norm2, self.seeded, self.knorm]
                    self.yT_low = c("yT_low")
                    self.vector.append(self.yT_low)
                    self.rsum, self.newton = c("rsum", 4), c("newton", 4 * NEWTON)
                    self.pool += [self.rsum, self.newton]

        CS, CC, CL = Counters("self"), Counters("cross"), Counters("local")

        def give_credit(eng, counted):
            for c in counted:
                eng.sem_inc(c.sem, CREDIT * c.k)

        class FeedForwardCounters:
            def __init__(self):
                def c(what, per_block=1):
                    return Counter(sem(f"ff_{what}"), per_block)

                self.shift_ps, self.xnT_ps, self.down_ps = c("shift_ps"), c("xnT_ps"), c("down_ps")
                self.up_gate, self.up_linear = c("up_gate", 3), c("up_linear", 3)
                self.tensor = [self.shift_ps, self.xnT_ps, self.down_ps, self.up_gate, self.up_linear]
                self.xnT, self.gelu = c("xnT"), c("gelu", 3)
                self.xnT_low = c("xnT_low")
                self.scalar = [self.xnT, self.gelu]
                self.bn1, self.bn2, self.cent, self.xn = c("bn1"), c("bn2"), c("cent"), c("xn")
                self.gate, self.upd = c("gate", 3), c("upd")
                self.vector = [self.bn1, self.bn2, self.cent, self.xn, self.gate, self.upd]
                self.eps, self.rstd = c("eps"), c("rstd")
                self.pool = [self.eps, self.rstd, self.xnT_low]

        CF = FeedForwardCounters()

        class Unit:
            def __init__(self, n, u, p):
                self.n, self.u, self.p = n, u, p

        class Turn:

            def __init__(self, base, v, parity, first=0, last=0):
                self.base, self.v, self.parity, self.first, self.last = base, v, parity, first, last

            def run(self, operation, lag, *part):
                if lag < self.first or lag > self.last:
                    return
                u = self.v - lag
                operation(Unit(self.base + u, u, (self.parity + lag) % 2), *part)

        def pipeline(eng, base, turn, lags, units=UNITS):
            for v in range(lags):
                turn(Turn(base, v, v % 2, last=v))
            hold(eng)
            with eng.Fori(0, (units - lags) // 2) as j:
                for p in range(2):
                    turn(Turn(base, j * 2 + (lags + p), p, last=lags))
            for v in range(units, units + lags):
                turn(Turn(base, v, v % 2, first=v - units + 1, last=lags))

        def cols(t, at, n):
            return t[:, bass.ds(at, n)]

        def hold(eng):
            eng.sem_inc(held, 1)

        PASSES_BEFORE_LAYERS = 5

        block = stack.enter_context(nc.Block())

        @block.sync
        def _(sp):
            for o in range(UNITS // NU):
                sp.dma_start(XA[:, o * NU * D:(o + 1) * NU * D].rearrange("t (b d) -> t b d", d=D),
                             x[o * NU:(o + 1) * NU].rearrange("b t d -> t b d")).then_inc(x_in[o], 16)
            for dst, src in ((ident, ident_in), (shift, shift_in), (rot, rot_in), (headmask, headmask_in),
                             (masks_f, masks_in)):
                sp.dma_start(dst[:, :], src).then_inc(consts_in, 16)
            sp.dma_start(WF[:, 0:4 * D], self_w).then_inc(selfw_in, 16)
            sp.dma_start(BO[:, :], self_bo).then_inc(selfw_in, 16)
            sp.dma_start(scl[:, :], qk_scale.to_broadcast([T, LAYERS * 2 * DH])).then_inc(consts_in, 16)
            sp.dma_start(W[:, :], cross_w).then_inc(attnw_in, 16)
            sp.dma_start(CTX[:, :].rearrange("t (b d) -> t b d", d=D), ctx_in.rearrange("b t d -> t b d")).then_inc(ctx_sem, 16)
            sp.wait_ge(pass_done, 2)
            sp.dma_start(WF[:, :], ffn_w[0]).then_inc(ffnw_in, 16)
            sp.wait_ge(pass_done, 4)
            sp.dma_start(W[:, :], attn_w[0]).then_inc(attnw_in, 16)
            with sp.Fori(1, LAYERS) as l:
                sp.wait_ge(pass_done, l * 2 + (PASSES_BEFORE_LAYERS - 1))
                sp.dma_start(W[:, :], attn_w[bass.ds(l, 1)].rearrange("o p n -> p (o n)")).then_inc(attnw_in, 16)
                sp.wait_ge(pass_done, l * 2 + PASSES_BEFORE_LAYERS)
                sp.dma_start(WF[:, :], ffn_w[bass.ds(l, 1)].rearrange("o p n -> p (o n)")).then_inc(ffnw_in, 16)
            sp.wait_ge(pass_done, PASSES_BEFORE_LAYERS + 2 * LAYERS + 1)
            sp.dma_start(out.rearrange("b t d -> t b d"), XA[:, :].rearrange("t (b d) -> t b d", d=D)).then_inc(out_sem, 16)
            sp.wait_ge(out_sem, 16)

        @block.gpsimd
        def _(pool):
            give_credit(pool, CS.pool + CC.pool + CL.pool)
            give_credit(pool, CF.pool)
            pool.memset(powc[:, :], -0.5).then_inc(const_made, 1)
            pool.memset(ones[:, :], 1.0).then_inc(const_made, 1)
            pool.memset(yT[:, :], 0.0).then_inc(const_made, 1)
            pool.memset(three_halves[:, :], 1.5).then_inc(const_made, 1)
            pool.wait_ge(const_made, 4)

            def norm_pass(k):
                mvv = mv[:, :].rearrange("t (u two) -> t u two", two=2)
                for q in range(UNITS // NU):
                    a, done = slice(q * NU, (q + 1) * NU), (k - 1) * (UNITS // NU) + q + 1
                    pool.wait_ge(ln_stats, done)
                    pool.tensor_scalar(rstd[:, a], mvv[:, a, 1], EPS, None, ALU.add).then_inc(ln_eps, 1)
                    pool.wait_ge(ln_eps, done)
                    pool.tensor_tensor(rstd[:, a], rstd[:, a], powc[:, a], ALU.pow).then_inc(ln_rstd, 1)

            def attention(C, kind, base, src, after):
                pool.wait_ge(pass_done, after)
                if kind == "cross":
                    pool.memset(QP[:, :], 0.0).then_inc(qp_zero, 1)
                    pool.wait_ge(ctx_sem, 16)

                def stage(w):
                    n, u = w.n, w.u
                    pool.wait_ge(C.xT_ps.sem, C.xT_ps.before(n, 1))
                    hold(pool)
                    i = pool.tensor_copy(xa[:, 0:D], cols(src, u * D, D))
                    if kind == "cross":
                        i = pool.tensor_copy(xa[:, D:2 * D], cols(CTX, u * D, D))
                    i.then_inc(C.staged.sem, 1)

                def rotate_sum(w, c):
                    n = w.n
                    pool.wait_ge(C.rotated.sem, C.rotated.of(n, c + 1))
                    if c < 2:
                        pool.wait_ge(C.trans_ps.sem, C.trans_ps.before(n, c + 1))
                    else:
                        pool.wait_ge(C.knorm.sem, C.knorm.before(n, c - 1))
                    t = tu[:, (c % 2) * 2 * BANK:(c % 2 + 1) * 2 * BANK].rearrange(
                        "t (w h s d) -> t w h s d", w=2, h=8, s=2)
                    r = rsb[:, c * BANK:(c + 1) * BANK].rearrange("t (h s d) -> t h s d", h=8, s=2)
                    pool.tensor_tensor(r[:, :, 0, :], t[:, 0, :, 0, :], t[:, 1, :, 1, :], ALU.add)
                    pool.tensor_tensor(r[:, :, 1, :], t[:, 0, :, 1, :], t[:, 1, :, 0, :], ALU.add)\
                        .then_inc(C.rsum.sem, 1)

                def rnorm(w):
                    n, p = w.n, w.p
                    pool.wait_ge(C.seeded.sem, C.seeded.of(n, 3))
                    y = guess[:, :]
                    for i in range(NEWTON):
                        if i:
                            pool.wait_ge(C.newton.sem, C.newton.of(n, 4 * i))
                        pool.tensor_tensor(newt[:, :], y, y, ALU.mult).then_inc(C.newton.sem, 1)
                        pool.wait_ge(C.newton.sem, C.newton.of(n, 4 * i + 1))
                        pool.tensor_tensor(newt[:, :], newt[:, :], n2h[:, :], ALU.mult).then_inc(C.newton.sem, 1)
                        pool.wait_ge(C.newton.sem, C.newton.of(n, 4 * i + 2))
                        pool.tensor_tensor(newt[:, :], newt[:, :], three_halves[:, :], ALU.add).then_inc(C.newton.sem, 1)
                        dst = y
                        if i == NEWTON - 1:
                            dst = rn[:, p * 2 * H:(p + 1) * 2 * H]
                            pool.wait_ge(C.prob.sem, C.prob.before(n, NG, 2))
                            pool.wait_ge(C.knorm.sem, C.knorm.before(n, 2, 2))
                        pool.wait_ge(C.newton.sem, C.newton.of(n, 4 * i + 3))
                        pool.tensor_tensor(dst, y, newt[:, :], ALU.mult).then_inc(C.newton.sem, 1)

                def normalise(w, g):
                    n = w.n
                    pool.wait_ge(C.recip.sem, C.recip.of(n, g + 1))
                    pv = P[:, g * BANK:(g + 1) * BANK].rearrange("t (h k) -> t h k", h=GH)
                    pool.tensor_tensor(pv, pv, ri[:, g * GH:(g + 1) * GH].unsqueeze(2).to_broadcast([T, GH, T]),
                                       ALU.mult).then_inc(C.probn.sem, 1)

                def turn_self(t):
                    t.run(normalise, 3, 0)
                    t.run(normalise, 3, 1)
                    t.run(normalise, 3, 2)
                    t.run(stage, 0)
                    t.run(normalise, 3, 3)

                def turn_cross(t):
                    t.run(normalise, 3, 0)
                    t.run(stage, 0)
                    t.run(normalise, 3, 1)
                    t.run(normalise, 3, 2)
                    t.run(normalise, 3, 3)

                def turn_local(t):
                    t.run(rotate_sum, 2, 2)
                    t.run(rotate_sum, 2, 3)
                    t.run(normalise, 3, 0)
                    t.run(rnorm, 2)
                    t.run(normalise, 3, 1)
                    t.run(rotate_sum, 1, 0)
                    t.run(normalise, 3, 2)
                    t.run(rotate_sum, 1, 1)
                    t.run(stage, 0)
                    t.run(normalise, 3, 3)

                turn_of_kind = {"self": turn_self, "cross": turn_cross, "local": turn_local}[kind]
                pipeline(pool, base, turn_of_kind, MAX_LAG[kind])

            def low_half(low, w, high, done):
                hold(pool)
                pool.tensor_tensor(low, w, high.bitcast(FP32), ALU.subtract).then_inc(done, 1)

            norm_pass(1)
            attention(CS, "self", 0, XB, 1)
            norm_pass(2)
            attention(CC, "cross", 0, XB, 3)
            norm_pass(3)
            pool.wait_ge(pass_done, PASSES_BEFORE_LAYERS)
            pool.memset(yT[:, 0:1], 0.0).then_inc(const_made, 1)
            pool.wait_ge(const_made, 5)
            pool.tensor_copy(yTh[:, 0:1], yT[:, 0:1])
            pool.tensor_copy(yTl[:, 0:1], yT[:, 0:1]).then_inc(const_made, 1)
            with pool.Fori(0, LAYERS) as l:
                pool.wait_ge(attnw_high, l + 1)
                low_half(W_low[:, 0:QKV], W[:, 0:QKV], W_high[:, :], attnw_split)
                attention(CL, "local", l * UNITS, XB, l * 2 + PASSES_BEFORE_LAYERS)
                pool.wait_ge(ffnw_in, l * 16 + 16)
                hold(pool)
                pool.tensor_copy(WF_high[:, 0:2 * FFP], WF[:, 0:2 * FFP]).then_inc(ffnw_high, 1)
                pool.wait_ge(ffnw_high, l + 1)
                low_half(WF_low[:, 0:2 * FFP], WF[:, 0:2 * FFP], WF_high[:, 0:2 * FFP], ffnw_split)
                pool.wait_ge(pass_done, l * 2 + (PASSES_BEFORE_LAYERS + 1))
                hold(pool)

                def make_rstd(w):
                    m = w.n
                    pool.wait_ge(CF.bn2.sem, CF.bn2.of(m, 1))
                    pool.wait_ge(CF.xn.sem, CF.xn.before(m, 1))
                    hold(pool)
                    mvv = mv[:, 0:2 * FB].rearrange("t (u two) -> t u two", two=2)
                    pool.tensor_scalar(rstd[:, 0:FB], mvv[:, :, 1], EPS, None, ALU.add).then_inc(CF.eps.sem, 1)
                    pool.wait_ge(CF.eps.sem, CF.eps.of(m, 1))
                    pool.tensor_tensor(rstd[:, 0:FB], rstd[:, 0:FB], powc[:, 0:FB], ALU.pow).then_inc(CF.rstd.sem, 1)

                def split_xnT(w):
                    m = w.n
                    half = slice(w.p * FB * T, (w.p + 1) * FB * T)
                    pool.wait_ge(CF.xnT.sem, CF.xnT.of(m, 1))
                    hold(pool)
                    pool.tensor_tensor(xnT_low[:, half], xnT[:, half], xnT_high[:, half].bitcast(FP32),
                                       ALU.subtract).then_inc(CF.xnT_low.sem, 1)

                def turn_ff(t):
                    t.run(make_rstd, 1)
                    t.run(split_xnT, 1)
                pipeline(pool, l * NFB, turn_ff, MAX_LAG["ff"], NFB)

        @block.scalar
        def _(act):
            give_credit(act, CS.scalar + CC.scalar + CL.scalar)
            give_credit(act, CF.scalar)
            act.wait_ge(const_made, 4)

            def attention(C, kind, base, after):
                act.wait_ge(pass_done, after)
                if kind == "cross":
                    act.wait_ge(qp_zero, 1)

                def evac_x(w):
                    n = w.n
                    act.wait_ge(C.xT_ps.sem, C.xT_ps.of(n, 1))
                    act.wait_ge(C.proj_ps.sem, C.proj_ps.before(n, C.proj_ps.k))
                    if kind == "local":
                        act.activation(yTh[0:64, 0:T], XTP[0:64, 0:T], ACT.Copy)
                        act.activation(yTh[64:128, 1:T], XTP[64:128, 0:T - 1], ACT.Copy)\
                           .then_inc(C.yT_sb.sem, 1)
                    else:
                        w = 2 * T if kind == "cross" else T
                        act.activation(yT[:, 0:w], TRP[:, 0:w], ACT.Copy).then_inc(C.yT_sb.sem, 1)

                def square(w, c):
                    n = w.n
                    act.wait_ge(C.proj_ps.sem, C.proj_ps.of(n, c + 1))
                    act.wait_ge(C.norm2.sem, C.norm2.of(n, c - 1) if c >= 2 else C.norm2.before(n, c + 3))
                    act.activation(sq[:, (c % 2) * BANK:(c % 2 + 1) * BANK], PROJ[c % 2][:, :], ACT.Square)\
                       .then_inc(C.squared.sem, 1)

                def store_q(n, p, c, src):
                    act.wait_ge(C.scores.sem, C.scores.before(n, NG, 2))
                    q = QP[:, p * H * T + c * 8 * T:p * H * T + (c + 1) * 8 * T].rearrange(
                        "f (i two t) -> f i two t", two=2, t=T)
                    s = src[:, :].rearrange("f (i t) -> f i t", t=T)
                    act.activation(q[0:64, :, 0, :], s[0:64], ACT.Copy)
                    act.activation(q[64:128, :, 1, :], s[64:128], ACT.Copy).then_inc(C.qk_sb.sem, 1)

                def store_k(n, p, c, src):
                    act.wait_ge(C.scores.sem, C.scores.before(n, NG, 2))
                    act.activation(KT[:, p * 8 * T + c * BANK:p * 8 * T + (c + 1) * BANK], src[:, :], ACT.Copy)\
                       .then_inc(C.qk_sb.sem, 1)

                def store_v(w, c):
                    n, p = w.n, w.p
                    act.wait_ge(C.proj_ps.sem, C.proj_ps.of(n, 4 + c + 1))
                    act.wait_ge(C.av_ps.sem, C.av_ps.before(n, NG, 2))
                    act.activation(V[:, p * H * D + c * BANK:p * H * D + (c + 1) * BANK], PROJ[c % 2][:, :], ACT.Copy)\
                       .then_inc(C.v_sb.sem, 1)

                def store_trans(w, i):
                    n, p = w.n, w.p
                    if kind == "local":
                        act.wait_ge(C.trans_ps.sem, C.trans_ps.of(n, i + 1))
                        src = TRP
                    else:
                        act.wait_ge(C.proj_ps.sem, C.proj_ps.of(n, i + 1))
                        src = PROJ[i % 2]
                    (store_q if i < 2 else store_k)(n, p, i % 2, src)

                def exps(w, g):
                    n, p = w.n, w.p
                    act.wait_ge(C.negmax.sem, C.negmax.of(n, g + 1))
                    act.wait_ge(C.probT_ps.sem, C.probT_ps.before(n, g + 1))
                    act.wait_ge(C.recip.sem, C.recip.before(n, g + 1))
                    for i in range(GH):
                        h = g * GH + i
                        scale = (rn[:, 2 * p * H + h:2 * p * H + h + 1] if kind == "local"
                                 else float((DH if kind == "cross" else DH_SELF) ** -0.5))
                        e = act.activation(P[:, h * T:(h + 1) * T], SPS[g % 2][:, i * T:(i + 1) * T], ACT.Exp,
                                           bias=nb[:, h:h + 1], scale=scale, accum_out=rs[:, h:h + 1])
                    e.then_inc(C.prob.sem, 1)

                def self_k(w):
                    n, p = w.n, w.p
                    act.wait_ge(C.proj_ps.sem, C.proj_ps.of(n, QKV_CHUNKS))
                    act.wait_ge(C.scores.sem, C.scores.before(n, NG, 2))
                    act.activation(KT[:, p * 8 * T:p * 8 * T + T], PROJ[1][:, 0:T], ACT.Copy).then_inc(C.selfk.sem, 1)

                def self_v(w):
                    n, p = w.n, w.p
                    act.wait_ge(C.proj_ps.sem, C.proj_ps.of(n, QKV_CHUNKS))
                    act.wait_ge(C.av_ps.sem, C.av_ps.before(n, NG, 2))
                    act.activation(V[:, p * H * D:(p + 1) * H * D].rearrange("t (h r d) -> t h r d", h=H, d=DH_SELF),
                                   PROJ[1][:, T:T + D].rearrange("t (h d) -> t h d", h=H).unsqueeze(2)
                                   .to_broadcast([T, H, D // DH_SELF, DH_SELF]), ACT.Copy).then_inc(C.selfv.sem, 1)

                def store_pT(w, g):
                    n = w.n
                    act.wait_ge(C.probT_ps.sem, C.probT_ps.of(n, g + 1))
                    act.wait_ge(C.av_ps.sem, C.av_ps.of(n, g - 1) if g >= 2 else C.av_ps.before(n, g + 3))
                    act.activation(PTs[:, (g % 2) * BANK:(g % 2 + 1) * BANK], PTP[:, :], ACT.Copy).then_inc(C.probT.sem, 1)

                def store_o(w, i):
                    n = w.n
                    act.wait_ge(C.av_ps.sem, C.av_ps.of(n, 2 * i + 2))
                    act.wait_ge(C.y_ps.sem, C.y_ps.before(n, 1))
                    act.activation(OT[:, i * BANK:(i + 1) * BANK], OTP[:, :], ACT.Copy).then_inc(C.oT_sb.sem, 1)

                def turn_self(t):
                    t.run(evac_x, 2)
                    t.run(exps, 3, 1)
                    t.run(store_pT, 3, 0)
                    t.run(exps, 3, 2)
                    t.run(self_k, 2)
                    t.run(store_pT, 3, 1)
                    t.run(exps, 3, 3)
                    t.run(self_v, 2)
                    t.run(store_pT, 3, 2)
                    t.run(exps, 2, 0)
                    t.run(store_pT, 3, 3)

                def turn_cross(t):
                    t.run(store_v, 2, 0)
                    t.run(evac_x, 1)
                    t.run(exps, 3, 2)
                    t.run(store_v, 2, 1)
                    t.run(store_trans, 1, 0)
                    t.run(exps, 3, 3)
                    t.run(store_trans, 1, 1)
                    t.run(store_o, 3, 0)
                    t.run(exps, 2, 0)
                    t.run(store_trans, 1, 2)
                    t.run(store_trans, 1, 3)
                    t.run(exps, 2, 1)
                    t.run(store_o, 3, 1)

                def turn_local(t):
                    t.run(square, 1, 1)
                    t.run(exps, 3, 1)
                    t.run(store_trans, 2, 1)
                    t.run(exps, 3, 2)
                    t.run(store_trans, 2, 2)
                    t.run(square, 1, 2)
                    t.run(store_trans, 2, 3)
                    t.run(exps, 3, 3)
                    t.run(store_o, 3, 0)
                    t.run(square, 1, 3)
                    t.run(store_trans, 1, 0)
                    t.run(exps, 2, 0)
                    t.run(evac_x, 0)
                    t.run(store_v, 1, 0)
                    t.run(store_v, 1, 1)
                    t.run(store_o, 3, 1)
                    t.run(square, 0, 0)

                turn_of_kind = {"self": turn_self, "cross": turn_cross, "local": turn_local}[kind]
                pipeline(act, base, turn_of_kind, MAX_LAG[kind])

            def store_xnT(w):
                m = w.n
                act.wait_ge(CF.xnT_ps.sem, CF.xnT_ps.of(m, 1))
                act.wait_ge(CF.xnT_low.sem, CF.xnT_low.before(m, 1, 2))
                act.wait_ge(CF.up_gate.sem, CF.up_gate.before(m, 3, 2))
                act.wait_ge(CF.up_linear.sem, CF.up_linear.before(m, 3, 2))
                half = slice(w.p * FB * T, (w.p + 1) * FB * T)
                gain, bias = WF[:, G_AT:G_AT + 1], WF[:, G_AT + 1:G_AT + 2]
                act.activation(xnT_high[:, half], TRP[:, :], ACT.Identity, bias=bias, scale=gain)
                act.activation(xnT[:, half], TRP[:, :], ACT.Identity, bias=bias, scale=gain).then_inc(CF.xnT.sem, 1)

            def gelu(w, c):
                m, r = w.n, FC[c]
                act.wait_ge(CF.up_gate.sem, CF.up_gate.of(m, c + 1))
                act.wait_ge(CF.gate.sem, CF.gate.before(m, c + 1))
                act.activation(gel[0:r, c * BANK:(c + 1) * BANK], GATES[c][0:r, :], ACT.Gelu,
                               bias=WF[0:r, B1_AT + 3 + c:B1_AT + 4 + c]).then_inc(CF.gelu.sem, 1)

            def turn_ff(t):
                t.run(gelu, 2, 0)
                t.run(gelu, 2, 1)
                t.run(gelu, 2, 2)
                t.run(store_xnT, 1)

            attention(CS, "self", 0, 1)
            attention(CC, "cross", 0, 3)
            act.wait_ge(const_made, 6)
            with act.Fori(0, LAYERS) as l:
                act.wait_ge(attnw_in, l * 16 + 32)
                act.activation(W_high[:, :], W[:, 0:QKV], ACT.Copy).then_inc(attnw_high, 1)
                attention(CL, "local", l * UNITS, l * 2 + PASSES_BEFORE_LAYERS)
                act.wait_ge(pass_done, l * 2 + (PASSES_BEFORE_LAYERS + 1))
                act.wait_ge(ffnw_in, l * 16 + 16)
                pipeline(act, l * NFB, turn_ff, MAX_LAG["ff"], NFB)

        @block.vector
        def _(dve):
            give_credit(dve, CS.vector + CC.vector + CL.vector)
            give_credit(dve, CF.vector)
            dve.wait_ge(consts_in, 16 * 6)
            dve.tensor_copy(identb[:, :], ident[:, :])
            dve.tensor_copy(masks[:, :], masks_f[:, :]).then_inc(bf_made, 1)

            def norm_pass(k, src, dst):
                def unit_stats(o):
                    for i in range(NU):
                        dve.bn_stats(cols(stats, o * (6 * NU) + i * 6, 6), cols(src, o * (NU * D) + i * D, D))\
                           .then_inc(ln_step, 1)

                if k == 1:
                    for o in range(UNITS // NU):
                        dve.wait_ge(x_in[o], 16)
                        unit_stats(o)
                else:
                    with dve.Fori(0, UNITS // NU) as o:
                        unit_stats(o)
                dve.wait_ge(ln_step, UNITS * (2 * k - 1))
                for u in range(UNITS):
                    b = dve.bn_aggr(mv[:, 2 * u:2 * u + 2], stats[:, 6 * u:6 * u + 6])
                    if u % NU == NU - 1:
                        b.then_inc(ln_stats, 1)
                with dve.Fori(0, UNITS // NU) as o:
                    dve.wait_ge(ln_rstd, o + ((k - 1) * (UNITS // NU) + 1))
                    for i in range(NU):
                        dve.tensor_scalar(cols(dst, o * (NU * D) + i * D, D), cols(src, o * (NU * D) + i * D, D),
                                          cols(mv, o * (2 * NU) + i * 2, 1), cols(rstd, o * NU + i, 1),
                                          ALU.subtract, ALU.mult).then_inc(ln_step, 1)
                dve.wait_ge(ln_step, UNITS * 2 * k)
                dve.sem_inc(pass_done, 1)

            def attention(C, kind, base, state):
                def evac_low(w):
                    n = w.n
                    dve.wait_ge(C.yT_sb.sem, C.yT_sb.of(n, 1))
                    dve.tensor_tensor(yTl[0:64, 0:T], XTP[0:64, 0:T], yTh[0:64, 0:T].bitcast(FP32), ALU.subtract)
                    dve.tensor_tensor(yTl[64:128, 1:T], XTP[64:128, 0:T - 1], yTh[64:128, 1:T].bitcast(FP32),
                                      ALU.subtract).then_inc(C.yT_low.sem, 1)

                def rotate(w, c):
                    n = w.n
                    dve.wait_ge(C.squared.sem, C.squared.of(n, c + 1))
                    dve.wait_ge(C.rsum.sem, C.rsum.of(n, c - 1) if c >= 2 else C.rsum.before(n, c + 3))
                    t = tu[:, (c % 2) * 2 * BANK:(c % 2 + 1) * 2 * BANK].rearrange("t (w h d) -> t w h d", w=2, h=8)
                    ps = PROJ[c % 2][:, :].rearrange("t (h d) -> t h d", h=8).unsqueeze(1).to_broadcast([T, 2, 8, DH])
                    a = (c // 2) * 2 * DH
                    tb = tab[:, a:a + 2 * DH].rearrange("t (w d) -> t w d", w=2).unsqueeze(2).to_broadcast([T, 2, 8, DH])
                    dve.tensor_tensor(t, ps, tb, ALU.mult).then_inc(C.rotated.sem, 1)

                def norm2(w, c):
                    n = w.n
                    dve.wait_ge(C.squared.sem, C.squared.of(n, c + 1))
                    dve.wait_ge(C.seeded.sem, C.seeded.before(n, 2))
                    dve.tensor_reduce(n2[:, c * 8:(c + 1) * 8],
                                      sq[:, (c % 2) * BANK:(c % 2 + 1) * BANK].rearrange("t (h d) -> t h d", h=8),
                                      AX.X, ALU.add).then_inc(C.norm2.sem, 1)

                def seed(w):
                    n = w.n
                    dve.wait_ge(C.norm2.sem, C.norm2.of(n, 4))
                    dve.wait_ge(C.newton.sem, C.newton.before(n, 4 * NEWTON))
                    dve.tensor_scalar(n2c[:, :], n2[:, :], 1e-24, None, ALU.max).then_inc(C.seeded.sem, 1)
                    dve.wait_ge(C.seeded.sem, C.seeded.of(n, 1))
                    dve.tensor_scalar(half_bits[:, :], n2c[:, :].bitcast(I32), 1, None, ALU.arith_shift_right)\
                       .then_inc(C.seeded.sem, 1)
                    dve.tensor_scalar(n2h[:, :], n2c[:, :], -0.5, None, ALU.mult)
                    dve.wait_ge(C.seeded.sem, C.seeded.of(n, 2))
                    dve.tensor_scalar(guess[:, :].bitcast(I32), half_bits[:, :], -1.0, float(MAGIC), ALU.mult, ALU.add)\
                       .then_inc(C.seeded.sem, 1)

                def knorm(w, c):
                    n = w.n
                    dve.wait_ge(C.newton.sem, C.newton.of(n, 4 * NEWTON))
                    dve.wait_ge(C.rsum.sem, C.rsum.of(n, 3 + c))
                    dve.wait_ge(C.trans_ps.sem, C.trans_ps.before(n, 3 + c))
                    dve.tensor_tensor(knb[:, c * BANK:(c + 1) * BANK].rearrange("t (h d) -> t h d", h=8),
                                      rsb[:, (2 + c) * BANK:(3 + c) * BANK].rearrange("t (h d) -> t h d", h=8),
                                      rn[:, (2 * w.p + 1) * H + c * 8:(2 * w.p + 1) * H + (c + 1) * 8].unsqueeze(2).to_broadcast([T, 8, DH]),
                                      ALU.mult).then_inc(C.knorm.sem, 1)

                def rowmax(w, g):
                    n, p = w.n, w.p
                    dve.wait_ge(C.scores.sem, C.scores.of(n, g + 1))
                    a = slice(g * GH, (g + 1) * GH)
                    dve.tensor_reduce(mx[:, a], SPS[g % 2][:, :].rearrange("t (h k) -> t h k", h=GH), AX.X,
                                      ALU.max).then_inc(C.rowmax.sem, 1)
                    dve.wait_ge(C.rowmax.sem, C.rowmax.of(n, g + 1))
                    dve.wait_ge(C.prob.sem, C.prob.before(n, g + 1))
                    if kind == "local":
                        dve.wait_ge(C.newton.sem, C.newton.of(n, 4 * NEWTON))
                        dve.scalar_tensor_tensor(out=nb[:, a], in0=mx[:, a], scalar=-1.0,
                                                 in1=rn[:, 2 * p * H + g * GH:2 * p * H + (g + 1) * GH],
                                                 op0=ALU.mult, op1=ALU.mult).then_inc(C.negmax.sem, 1)
                    else:
                        s = float((DH if kind == "cross" else DH_SELF) ** -0.5)
                        dve.tensor_scalar(nb[:, a], mx[:, a], -s, None, ALU.mult).then_inc(C.negmax.sem, 1)

                def recip(w, g):
                    n = w.n
                    dve.wait_ge(C.prob.sem, C.prob.of(n, g + 1))
                    dve.wait_ge(C.probn.sem, C.probn.before(n, g + 1))
                    a = slice(g * GH, (g + 1) * GH)
                    dve.reciprocal(ri[:, a], rs[:, a]).then_inc(C.recip.sem, 1)

                def store_pT(w, g):
                    n = w.n
                    dve.wait_ge(C.probT_ps.sem, C.probT_ps.of(n, g + 1))
                    dve.wait_ge(C.av_ps.sem, C.av_ps.of(n, g - 1) if g >= 2 else C.av_ps.before(n, g + 3))
                    dve.tensor_copy(PTs[:, (g % 2) * BANK:(g % 2 + 1) * BANK], PTP[:, :]).then_inc(C.probT.sem, 1)

                def self_q(w):
                    n, p = w.n, w.p
                    dve.wait_ge(C.proj_ps.sem, C.proj_ps.of(n, QKV_CHUNKS))
                    dve.wait_ge(C.scores.sem, C.scores.before(n, NG, 2))
                    dve.tensor_tensor(QP[:, p * H * T:(p + 1) * H * T].rearrange("f (h t) -> f h t", h=H),
                                      PROJ[0][:, 0:T].unsqueeze(1).to_broadcast([128, H, T]),
                                      headmask[:, :].unsqueeze(2).to_broadcast([128, H, T]), ALU.mult)\
                       .then_inc(C.selfq.sem, 1)

                def pick(w, g):
                    n = w.n
                    dve.wait_ge(C.av_ps.sem, C.av_ps.of(n, g + 1))
                    s = sq[:, (g % 2) * BANK:(g % 2 + 1) * BANK]
                    dve.tensor_tensor(s.rearrange("f (a r) -> f a r", r=D // DH_SELF),
                                      OTP[:, :].rearrange("f (a r) -> f a r", r=D // DH_SELF),
                                      headmask[:, :].unsqueeze(1).to_broadcast([128, BANK // H, H]), ALU.mult)\
                       .then_inc(C.picked.sem, 1)
                    dve.wait_ge(C.picked.sem, C.picked.of(n, g + 1))
                    dve.wait_ge(C.y_ps.sem, C.y_ps.before(n, 1))
                    w = BANK // H
                    dve.tensor_reduce(OT[:, g * w:(g + 1) * w], s.rearrange("f (a r) -> f a r", r=D // DH_SELF),
                                      AX.X, ALU.add).then_inc(C.selfo.sem, 1)

                def update(w):
                    n, u = w.n, w.u
                    dve.wait_ge(C.y_ps.sem, C.y_ps.of(n, 1))
                    dve.tensor_tensor(cols(state, u * D, D), cols(state, u * D, D), RESULT[kind], ALU.add)\
                       .then_inc(C.updated.sem, 1)

                def turn_self(t):
                    t.run(recip, 3, 3)
                    t.run(rowmax, 2, 0)
                    t.run(pick, 3, 1)
                    t.run(rowmax, 2, 1)
                    t.run(recip, 2, 0)
                    t.run(pick, 3, 2)
                    t.run(rowmax, 2, 2)
                    t.run(recip, 2, 1)
                    t.run(pick, 3, 3)
                    t.run(rowmax, 2, 3)
                    t.run(recip, 2, 2)
                    t.run(self_q, 1)
                    t.run(pick, 2, 0)
                    t.run(update, 3)

                def turn_cross(t):
                    t.run(store_pT, 3, 1)
                    t.run(store_pT, 3, 2)
                    t.run(rowmax, 2, 0)
                    t.run(recip, 3, 3)
                    t.run(rowmax, 2, 1)
                    t.run(store_pT, 3, 3)
                    t.run(recip, 2, 0)
                    t.run(rowmax, 2, 2)
                    t.run(recip, 2, 1)
                    t.run(recip, 2, 2)
                    t.run(store_pT, 2, 0)
                    t.run(update, 3)
                    t.run(rowmax, 2, 3)

                def turn_local(t):
                    t.run(knorm, 2, 1)
                    t.run(recip, 3, 2)
                    t.run(store_pT, 3, 1)
                    t.run(rowmax, 3, 3)
                    t.run(norm2, 1, 1)
                    t.run(rotate, 1, 2)
                    t.run(store_pT, 3, 2)
                    t.run(recip, 3, 3)
                    t.run(rowmax, 2, 0)
                    t.run(rotate, 1, 3)
                    t.run(norm2, 1, 2)
                    t.run(store_pT, 3, 3)
                    t.run(norm2, 1, 3)
                    t.run(recip, 2, 0)
                    t.run(evac_low, 0)
                    t.run(seed, 1)
                    t.run(rowmax, 2, 1)
                    t.run(rowmax, 2, 2)
                    t.run(rotate, 0, 0)
                    t.run(norm2, 0, 0)
                    t.run(rotate, 0, 1)
                    t.run(recip, 2, 1)
                    t.run(knorm, 1, 0)
                    t.run(store_pT, 2, 0)
                    t.run(update, 3)

                turn_of_kind = {"self": turn_self, "cross": turn_cross, "local": turn_local}[kind]
                pipeline(dve, base, turn_of_kind, MAX_LAG[kind])
                dve.wait_ge(C.updated.sem, C.updated.of(base + (UNITS - 1), 1))
                dve.sem_inc(pass_done, 1)

            def block_of(w):
                return cols(XB, w.u * (FB * D), FB * D)

            def statistics(w):
                m = w.n
                dve.wait_ge(CF.shift_ps.sem, CF.shift_ps.of(m, 1))
                dve.wait_ge(CF.rstd.sem, CF.rstd.before(m, 1))
                dve.wait_ge(CF.cent.sem, CF.cent.before(m, 1))
                st = stats[:, 0:FB * 12].rearrange("t (u s) -> t u s", s=12)
                for u in range(FB):
                    dve.bn_stats(st[:, u, 0:6], cols(XB, w.u * (FB * D) + u * D, 64))
                    b = dve.bn_stats(st[:, u, 6:12], YPS[:, u * 64:(u + 1) * 64])
                b.then_inc(CF.bn1.sem, 1)
                dve.wait_ge(CF.bn1.sem, CF.bn1.of(m, 1))
                hold(dve)
                for u in range(FB):
                    b = dve.bn_aggr(mv[:, 2 * u:2 * u + 2], st[:, u, :])
                b.then_inc(CF.bn2.sem, 1)

            def center(w):
                m = w.n
                dve.wait_ge(CF.bn2.sem, CF.bn2.of(m, 1))
                dve.wait_ge(CF.xn.sem, CF.xn.before(m, 1))
                blk = block_of(w).rearrange("t (u d) -> t u d", u=FB)
                mean = mv[:, 0:2 * FB].rearrange("t (u two) -> t u two", two=2)[:, :, 0:1].to_broadcast([T, FB, 64])
                xcv = xc[:, :].rearrange("t (u d) -> t u d", u=FB)
                dve.tensor_tensor(xcv[:, :, 0:64], blk[:, :, 0:64], mean, ALU.subtract)
                dve.tensor_tensor(xcv[:, :, 64:128], YPS[:, 0:FB * 64].rearrange("t (u d) -> t u d", u=FB), mean,
                                  ALU.subtract).then_inc(CF.cent.sem, 1)

            def make_xn(w):
                m = w.n
                dve.wait_ge(CF.cent.sem, CF.cent.of(m, 1))
                dve.wait_ge(CF.rstd.sem, CF.rstd.of(m, 1))
                dve.wait_ge(CF.xnT_ps.sem, CF.xnT_ps.before(m, 1))
                dve.tensor_tensor(xn[:, :].rearrange("t (u d) -> t u d", u=FB),
                                  xc[:, :].rearrange("t (u d) -> t u d", u=FB),
                                  rstd[:, 0:FB].unsqueeze(2).to_broadcast([T, FB, D]), ALU.mult).then_inc(CF.xn.sem, 1)

            def gate(w, c):
                m, r = w.n, FC[c]
                dve.wait_ge(CF.gelu.sem, CF.gelu.of(m, c + 1))
                dve.wait_ge(CF.up_linear.sem, CF.up_linear.of(m, c + 1))
                dve.wait_ge(CF.down_ps.sem, CF.down_ps.before(m, 1))
                a = slice(c * BANK, (c + 1) * BANK)
                dve.scalar_tensor_tensor(out=gT[0:r, a], in0=PROJ[c % 2][0:r, :],
                                         scalar=WF[0:r, B1_AT + c:B1_AT + c + 1], in1=gel[0:r, a],
                                         op0=ALU.add, op1=ALU.mult).then_inc(CF.gate.sem, 1)

            def ff_update(w):
                m = w.n
                dve.wait_ge(CF.down_ps.sem, CF.down_ps.of(m, 1))
                dve.tensor_tensor(block_of(w), block_of(w), PTP[:, :], ALU.add).then_inc(CF.upd.sem, 1)

            def turn_ff(t):
                t.run(gate, 2, 0)
                t.run(make_xn, 1)
                t.run(gate, 2, 1)
                t.run(gate, 2, 2)
                t.run(statistics, 0)
                t.run(ff_update, 2)
                t.run(center, 0)

            norm_pass(1, XA, XB)
            attention(CS, "self", 0, XA)
            norm_pass(2, XA, XB)
            attention(CC, "cross", 0, XA)
            norm_pass(3, XA, XB)
            dve.wait_ge(const_made, 6)
            with dve.Fori(0, LAYERS) as l:
                dve.tensor_tensor(tab[:, :].rearrange("t (w s d) -> t w s d", w=2, s=2),
                                  rot[:, :].rearrange("t (w s d) -> t w s d", w=2, s=2),
                                  cols(scl, l * (2 * DH), 2 * DH).rearrange("t (w d) -> t w d", w=2).unsqueeze(2)
                                  .to_broadcast([T, 2, 2, DH]), ALU.mult).then_inc(tab_made, 1)
                dve.wait_ge(tab_made, l + 1)
                attention(CL, "local", l * UNITS, XB)
                dve.wait_ge(ffnw_in, l * 16 + 16)
                hold(dve)
                pipeline(dve, l * NFB, turn_ff, MAX_LAG["ff"], NFB)
                dve.wait_ge(CF.upd.sem, CF.upd.of(l * NFB + (NFB - 1), 1))
                dve.sem_inc(pass_done, 1)
            dve.tensor_tensor(XA[:, :], XA[:, :], XB[:, :], ALU.add).then_inc(pass_done, 1)

        @block.tensor
        def _(pe):
            give_credit(pe, CS.tensor + CC.tensor + CL.tensor)
            give_credit(pe, CF.tensor)
            pe.wait_ge(consts_in, 16 * 6)
            pe.wait_ge(const_made, 4)
            pe.wait_ge(bf_made, 1)

            def product(out, a_high, a_low, b_high, b_low):
                pe.matmul(out, a_high, b_high, start=True, stop=False)
                pe.matmul(out, a_high, b_low, start=False, stop=False)
                return pe.matmul(out, a_low, b_high, start=False, stop=True)

            def attention(C, kind, base, after):
                pe.wait_ge(pass_done, after)

                def transpose_x(w):
                    n = w.n
                    pe.wait_ge(C.staged.sem, C.staged.of(n, 1))
                    if kind == "local":
                        pe.wait_ge(C.yT_low.sem, C.yT_low.before(n, 1))
                        pe.transpose(XTP, xa[:, 0:D], ident[:, :]).then_inc(C.xT_ps.sem, 1)
                        return
                    else:
                        pe.wait_ge(C.yT_sb.sem, C.yT_sb.before(n, 1))
                    i = pe.transpose(TRP[:, 0:T], xa[:, 0:D], ident[:, :])
                    if kind == "cross":
                        i = pe.transpose(TRP[:, T:2 * T], xa[:, D:2 * D], ident[:, :])
                    i.then_inc(C.xT_ps.sem, 1)

                def project_self(w):
                    n = w.n
                    pe.wait_ge(C.yT_sb.sem, C.yT_sb.of(n, 1))
                    pe.wait_ge(C.selfq.sem, C.selfq.before(n, 1))
                    pe.wait_ge(C.selfv.sem, C.selfv.before(n, 1))
                    pe.wait_ge(C.selfk.sem, C.selfk.before(n, 1))
                    pe.matmul(PROJ[0][:, 0:T], WF[:, 0:D], yT[:, 0:T], start=True, stop=True)
                    pe.matmul(PROJ[1][:, T:T + D], yT[:, 0:T], WF[:, 2 * D:3 * D], start=True, stop=True)
                    pe.matmul(PROJ[1][:, 0:T], WF[:, D:2 * D], yT[:, 0:T], start=True, stop=True)\
                      .then_inc(C.proj_ps.sem, QKV_CHUNKS)

                def project(w, c):
                    n = w.n
                    if c == 0 and kind == "local":
                        pe.wait_ge(C.yT_low.sem, C.yT_low.of(n, 1))
                    elif c == 0:
                        pe.wait_ge(C.yT_sb.sem, C.yT_sb.of(n, 1))
                    if c < 2:
                        pe.wait_ge(C.v_sb.sem, C.v_sb.before(n, c + 1))
                    elif kind == "local":
                        pe.wait_ge(C.rotated.sem, C.rotated.of(n, c - 1))
                    else:
                        pe.wait_ge(C.qk_sb.sem, C.qk_sb.of(n, c - 1))
                    chunk = slice(c * BANK, (c + 1) * BANK)
                    if kind == "local":
                        product(PROJ[c % 2][:, :], yTh[:, :], yTl[:, :], W_high[:, chunk], W_low[:, chunk])\
                            .then_inc(C.proj_ps.sem, 1)
                        return
                    if c >= 4:
                        pe.matmul(PROJ[c % 2][:, :], yT[:, T:2 * T], W[:, chunk],
                                  start=True, stop=True).then_inc(C.proj_ps.sem, 1)
                        return
                    a = T if c >= 2 else 0
                    for i in range(4):
                        o = c * BANK + i * 128
                        mm = pe.matmul(PROJ[c % 2][:, i * T:(i + 1) * T], W[:, o:o + 128], yT[:, a:a + T],
                                       start=True, stop=True)
                    mm.then_inc(C.proj_ps.sem, 1)

                def transpose_qk(w, i):
                    n = w.n
                    if i < 2:
                        pe.wait_ge(C.rsum.sem, C.rsum.of(n, i + 1))
                    else:
                        pe.wait_ge(C.knorm.sem, C.knorm.of(n, i - 1))
                    pe.wait_ge(C.qk_sb.sem, C.qk_sb.of(n, i) if i else C.qk_sb.before(n, 4))
                    src = rsb[:, i * BANK:(i + 1) * BANK] if i < 2 else knb[:, (i - 2) * BANK:(i - 1) * BANK]
                    for j in range(4):
                        t = pe.transpose(TRP[:, j * T:(j + 1) * T], src[:, j * 128:(j + 1) * 128], ident[:, :])
                    t.then_inc(C.trans_ps.sem, 1)

                def scores(w, g):
                    n, p = w.n, w.p
                    if g == 0 and kind == "local":
                        pe.wait_ge(C.qk_sb.sem, C.qk_sb.of(n, 4))
                    elif g == 0 and kind == "self":
                        pe.wait_ge(C.selfq.sem, C.selfq.of(n, 1))
                        pe.wait_ge(C.selfk.sem, C.selfk.of(n, 1))
                    elif g == 0:
                        pe.wait_ge(C.qk_sb.sem, C.qk_sb.of(n, 4))
                    pe.wait_ge(C.prob.sem, C.prob.of(n, g - 1) if g >= 2 else C.prob.before(n, g + 3))
                    bank = SPS[g % 2]
                    masked = kind != "cross"
                    if masked:
                        a = 0 if kind == "self" else T
                        pe.matmul(bank[:, :].rearrange("t (h k) -> t h k", h=GH), identb[:, :],
                                  masks[:, a:a + T].unsqueeze(1).to_broadcast([128, GH, T]), start=True, stop=False)
                    for i in range(GH):
                        h = g * GH + i
                        c = 0 if kind == "self" else h // 2
                        mm = pe.matmul(bank[:, i * T:(i + 1) * T], QP[:, (p * H + h) * T:(p * H + h + 1) * T],
                                       KT[:, (p * 8 + c) * T:(p * 8 + c + 1) * T],
                                       start=not masked, stop=(not masked or i == GH - 1))
                    mm.then_inc(C.scores.sem, 1)

                def transpose_p(w, g):
                    n = w.n
                    pe.wait_ge(C.probn.sem, C.probn.of(n, g + 1))
                    pe.wait_ge(C.probT.sem, C.probT.of(n, g) if g else C.probT.before(n, NG))
                    for i in range(GH):
                        h = g * GH + i
                        t = pe.transpose(PTP[:, i * T:(i + 1) * T], P[:, h * T:(h + 1) * T], ident[:, :])
                    t.then_inc(C.probT_ps.sem, 1)

                def weigh_v(w, g):
                    n, p = w.n, w.p
                    pe.wait_ge(C.probT.sem, C.probT.of(n, g + 1))
                    if kind == "self":
                        if g == 0:
                            pe.wait_ge(C.selfv.sem, C.selfv.of(n, 1))
                        pe.wait_ge(C.picked.sem, C.picked.of(n, g) if g else C.picked.before(n, NG))
                    elif g % 2 == 0:
                        pe.wait_ge(C.v_sb.sem, C.v_sb.of(n, g // 2 + 1))
                        if g:
                            pe.wait_ge(C.oT_sb.sem, C.oT_sb.of(n, 1))
                        else:
                            pe.wait_ge(C.updated.sem, C.updated.before(n, 1))
                    for i in range(GH):
                        h = g * GH + i
                        pt = PTs[:, (g % 2) * BANK + i * T:(g % 2) * BANK + (i + 1) * T]
                        if kind == "self":
                            mm = pe.matmul(OTP[:, i * T:(i + 1) * T], V[:, (p * H + h) * D:(p * H + h + 1) * D],
                                           pt, start=True, stop=True)
                        else:
                            r, c = (h % 2) * 64, (h % 8) // 2
                            v0 = p * H * D + h * DH
                            mm = pe.matmul(OTP[r:r + 64, c * T:(c + 1) * T], V[:, v0:v0 + DH], pt,
                                           start=True, stop=True)
                    mm.then_inc(C.av_ps.sem, 1)

                def project_out(w):
                    n = w.n
                    if kind == "self":
                        pe.wait_ge(C.selfo.sem, C.selfo.of(n, NG))
                    else:
                        pe.wait_ge(C.oT_sb.sem, C.oT_sb.of(n, 2))
                    if kind == "self":
                        pe.wait_ge(C.updated.sem, C.updated.before(n, 1))
                        pe.matmul(YPS[:, 0:D], ones[:, :], BO[:, :], start=True, stop=False)
                        pe.matmul(YPS[:, 0:D], OT[:, 0:T], WF[:, 3 * D:4 * D], start=False, stop=True)\
                          .then_inc(C.y_ps.sem, 1)
                        return
                    for c in range(8):
                        mm = pe.matmul(RESULT[kind], OT[:, c * T:(c + 1) * T], W[:, WO_AT + c * D:WO_AT + (c + 1) * D],
                                       start=c == 0, stop=c == 7)
                    mm.then_inc(C.y_ps.sem, 1)

                def turn_self(t):
                    t.run(transpose_p, 3, 2)
                    t.run(scores, 2, 0)
                    t.run(weigh_v, 3, 1)
                    t.run(scores, 2, 1)
                    t.run(transpose_p, 3, 3)
                    t.run(weigh_v, 3, 2)
                    t.run(scores, 2, 2)
                    t.run(transpose_p, 2, 0)
                    t.run(weigh_v, 3, 3)
                    t.run(scores, 2, 3)
                    t.run(project_self, 1)
                    t.run(transpose_p, 2, 1)
                    t.run(project_out, 3)
                    t.run(weigh_v, 2, 0)
                    t.run(transpose_x, 0)

                def turn_cross(t):
                    t.run(transpose_x, 0)
                    t.run(transpose_p, 3, 0)
                    t.run(scores, 3, 3)
                    t.run(scores, 2, 0)
                    t.run(transpose_p, 3, 1)
                    t.run(weigh_v, 3, 0)
                    t.run(project, 1, 1)
                    t.run(transpose_p, 3, 2)
                    t.run(weigh_v, 3, 1)
                    t.run(project, 1, 2)
                    t.run(scores, 2, 1)
                    t.run(project, 1, 3)
                    t.run(transpose_p, 3, 3)
                    t.run(weigh_v, 3, 2)
                    t.run(scores, 2, 2)
                    t.run(weigh_v, 3, 3)
                    t.run(project, 1, 4)
                    t.run(project, 1, 5)
                    t.run(project_out, 3)
                    t.run(project, 0, 0)

                def turn_local(t):
                    t.run(scores, 3, 3)
                    t.run(project, 1, 2)
                    t.run(transpose_qk, 2, 2)
                    t.run(transpose_p, 3, 1)
                    t.run(project, 1, 3)
                    t.run(transpose_qk, 2, 3)
                    t.run(weigh_v, 3, 0)
                    t.run(weigh_v, 3, 1)
                    t.run(transpose_p, 3, 2)
                    t.run(scores, 2, 0)
                    t.run(transpose_qk, 1, 0)
                    t.run(project, 1, 4)
                    t.run(transpose_x, 0)
                    t.run(scores, 2, 1)
                    t.run(transpose_p, 3, 3)
                    t.run(project, 1, 5)
                    t.run(weigh_v, 3, 2)
                    t.run(weigh_v, 3, 3)
                    t.run(scores, 2, 2)
                    t.run(project, 0, 0)
                    t.run(project, 0, 1)
                    t.run(transpose_p, 2, 0)
                    t.run(transpose_qk, 1, 1)
                    t.run(project_out, 3)

                turn_of_kind = {"self": turn_self, "cross": turn_cross, "local": turn_local}[kind]
                pipeline(pe, base, turn_of_kind, MAX_LAG[kind])

            def shift_state(w):
                m = w.n
                pe.wait_ge(CF.cent.sem, CF.cent.before(m, 1))
                blk = cols(XB, w.u * (FB * D), FB * D).rearrange("t (u d) -> t u d", u=FB)
                pe.matmul(YPS[:, 0:FB * 64].rearrange("t (u d) -> t u d", u=FB), shift[:, :], blk[:, :, 64:128],
                          start=True, stop=True).then_inc(CF.shift_ps.sem, 1)

            def transpose_xn(w):
                m = w.n
                pe.wait_ge(CF.xn.sem, CF.xn.of(m, 1))
                pe.wait_ge(CF.xnT.sem, CF.xnT.before(m, 1))
                for u in range(FB):
                    t = pe.transpose(TRP[:, u * T:(u + 1) * T], xn[:, u * D:(u + 1) * D], ident[:, :])
                t.then_inc(CF.xnT_ps.sem, 1)

            def up(w, c, half, bank):
                m = w.n
                if c == 0:
                    pe.wait_ge(CF.xnT_low.sem, CF.xnT_low.of(m, 1))
                tokens = slice(w.p * FB * T, (w.p + 1) * FB * T)
                chunk = slice(half * FFP + c * 128, half * FFP + (c + 1) * 128)
                return product(bank[:, :], WF_high[:, chunk], WF_low[:, chunk], xnT_high[:, tokens], xnT_low[:, tokens])

            def up_gate(w, c):
                pe.wait_ge(CF.gelu.sem, CF.gelu.before(w.n, c + 1))
                up(w, c, 1, GATES[c]).then_inc(CF.up_gate.sem, 1)

            def up_linear(w, c):
                pe.wait_ge(CF.gate.sem, CF.gate.of(w.n, 1) if c == 2 else CF.gate.before(w.n, [3, 2][c]))
                up(w, c, 0, PROJ[c % 2]).then_inc(CF.up_linear.sem, 1)

            def down(w):
                m = w.n
                pe.wait_ge(CF.gate.sem, CF.gate.of(m, 3))
                pe.wait_ge(CF.upd.sem, CF.upd.before(m, 1))
                pe.matmul(PTP[:, :].rearrange("t (u d) -> t u d", u=FB), ones[:, :],
                          WF[0:1, B2_AT:B2_AT + D].unsqueeze(1).to_broadcast([1, FB, D]), start=True, stop=False)
                for u in range(FB):
                    for c, r in enumerate(FC):
                        mm = pe.matmul(PTP[:, u * D:(u + 1) * D], gT[0:r, c * BANK + u * T:c * BANK + (u + 1) * T],
                                       WF[0:r, W2_AT + c * D:W2_AT + (c + 1) * D], start=False,
                                       stop=(u == FB - 1 and c == 2))
                mm.then_inc(CF.down_ps.sem, 1)

            def turn_ff(t):
                t.run(transpose_xn, 1)
                t.run(shift_state, 0)
                t.run(down, 2)
                t.run(up_gate, 1, 0)
                t.run(up_linear, 1, 0)
                t.run(up_gate, 1, 1)
                t.run(up_gate, 1, 2)
                t.run(up_linear, 1, 1)
                t.run(up_linear, 1, 2)

            pe.wait_ge(selfw_in, 32)
            attention(CS, "self", 0, 1)
            pe.wait_ge(attnw_in, 16)
            attention(CC, "cross", 0, 3)
            with pe.Fori(0, LAYERS) as l:
                pe.wait_ge(attnw_split, l + 1)
                attention(CL, "local", l * UNITS, l * 2 + PASSES_BEFORE_LAYERS)
                pe.wait_ge(pass_done, l * 2 + (PASSES_BEFORE_LAYERS + 1))
                pe.wait_ge(ffnw_split, l + 1)
                hold(pe)
                pipeline(pe, l * NFB, turn_ff, MAX_LAG["ff"], NFB)


def constants():
    import numpy as np
    f = np.float32
    half = np.arange(0, DH, 2, dtype=f)
    inv_freq = f(1.0) / f(10000.0) ** (half / f(DH))
    t = np.arange(T, dtype=f)
    freqs = t[:, None] * inv_freq[None, :]
    base = (half + f(0.4 * DH)) / f(1.4 * DH)
    power = (t - T // 2) / f(16)
    scale = base[None, :] ** power[:, None]
    cos, sin = np.cos(freqs), np.sin(freqs)
    parts = []
    for s in (scale * f(QK_SCALE), f(1.0) / scale):
        parts += [cos * s, cos * s, sin * s, -sin * s]
    rot = np.concatenate(parts, 1).astype(f)
    ident = np.eye(128, dtype=f)
    shift = np.eye(128, k=1, dtype=f)
    i, j = np.arange(T)[:, None], np.arange(T)[None, :]
    far = f(-1e30)
    causal = np.where(j > i, far, f(0))
    band = np.where((j > i) | (i - j > 32), far, f(0))
    masks = np.concatenate([causal, band], 1).astype(f)
    head = np.arange(D) // DH_SELF
    headmask = (head[:, None] == np.arange(H)[None, :]).astype(f)
    return ident, shift, rot, headmask, masks


def kernel(x, ctx_1024, L0_attn_Wq, L0_attn_Wk, L0_attn_Wv, L0_attn_Wo, L0_attn_bo, L0_xattn_Wq, L0_xattn_Wk,
           L0_xattn_Wv, L0_xattn_Wo, L0_ffn_Wqkv, L0_ffn_q_scale, L0_ffn_k_scale, L0_ffn_Wo, L0_ffn_ln_g,
           L0_ffn_ln_b, L0_ffn_W1, L0_ffn_b1, L0_ffn_W2, L0_ffn_b2):
    import numpy as np
    import concourse.bacc as bacc
    from concourse.bass_utils import run_bass_kernel_spmd

    def rows(w):
        w = np.asarray(w)
        return w.reshape(-1, 128, w.shape[-1]).transpose(1, 0, 2).reshape(128, -1)

    A = np.asarray
    self_w = np.concatenate([A(L0_attn_Wq), A(L0_attn_Wk), A(L0_attn_Wv), A(L0_attn_Wo)], 1)
    cross_w = np.concatenate([A(L0_xattn_Wq), A(L0_xattn_Wk), A(L0_xattn_Wv), rows(L0_xattn_Wo)], 1)
    attn_w = np.stack([np.concatenate([A(L0_ffn_Wqkv)[l], rows(A(L0_ffn_Wo)[l])], 1) for l in range(LAYERS)])
    qk_scale = np.concatenate([A(L0_ffn_q_scale), A(L0_ffn_k_scale)], 1).reshape(1, -1)
    ffn_w = np.zeros((LAYERS, 128, FFN_COLS), A(L0_ffn_W1).dtype)
    for l in range(LAYERS):
        ffn_w[l, :, 0:FF] = A(L0_ffn_W1)[l][:, 0:FF]
        ffn_w[l, :, FFP:FFP + FF] = A(L0_ffn_W1)[l][:, FF:2 * FF]
        for c, w in enumerate(FC):
            ffn_w[l, 0:w, W2_AT + c * D:W2_AT + (c + 1) * D] = A(L0_ffn_W2)[l, c * 128:c * 128 + w]
            ffn_w[l, 0:w, B1_AT + c] = A(L0_ffn_b1)[l, c * 128:c * 128 + w]
            ffn_w[l, 0:w, B1_AT + 3 + c] = A(L0_ffn_b1)[l, FF + c * 128:FF + c * 128 + w]
        ffn_w[l, :, G_AT] = A(L0_ffn_ln_g)[l]
        ffn_w[l, :, G_AT + 1] = A(L0_ffn_ln_b)[l]
        ffn_w[l, 0, B2_AT:B2_AT + D] = A(L0_ffn_b2)[l]
    ident, shift, rot, headmask, masks = constants()
    arrays = {
        "x": x, "ctx": ctx_1024, "self_w": self_w, "self_bo": A(L0_attn_bo).reshape(1, D), "cross_w": cross_w,
        "attn_w": attn_w, "qk_scale": qk_scale, "ffn_w": ffn_w, "ident": ident, "shift": shift, "rot": rot,
        "headmask": headmask, "masks": masks,
    }
    nc = bacc.Bacc("TRN2", target_bir_lowering=False, num_devices=1)
    feeds, args = {}, []
    for name, a in arrays.items():
        a = np.ascontiguousarray(a)
        feeds[f"{name}_dram"] = a
        args.append(nc.dram_tensor(f"{name}_dram", a.shape, mybir.dt.from_np(a.dtype), kind="ExternalInput").ap())
    args.append(nc.dram_tensor("out_dram", (UNITS, T, D), FP32, kind="ExternalOutput").ap())
    build(nc, *args)
    r = run_bass_kernel_spmd(nc, [feeds], core_ids=[0])
    return r.results[0]["out_dram"]
```
